# Optimizing a Trainium2 kernel written in Bass

```python
import numpy as np
import jax
import jax.numpy as jnp

def _softmax(x, axis=-1):
    return jax.nn.softmax(x, axis=axis)

def _gelu(x):
    return jax.nn.gelu(x, approximate=True)

def _silu(x):
    return jax.nn.silu(x)

def _sigmoid(x):
    return jax.nn.sigmoid(x)

def _layernorm(x, axis=-1, eps=1e-05):
    m = jnp.mean(x, axis=axis, keepdims=True)
    v = jnp.var(x, axis=axis, keepdims=True)
    return (x - m) / jnp.sqrt(v + eps)

def _scatter_add(tgt, idx, src, axis=0):
    return tgt.at[idx].add(src)

def _segment_sum(src, seg, n):
    return jax.ops.segment_sum(src, seg, n)
kernel_name = 'mk_gnn_resnorm_d4_gnn_r64_e04339'

def setup_inputs(seed: int=0):
    np.random.seed(seed)
    _w = jnp.asarray

    def _rec_inputs():
        import jax
        import jax.numpy as jnp
        _gk = jax.random.key(seed)
        x = -0.0002117 + 1 * jax.random.normal(jax.random.fold_in(_gk, 1), (50000, 256), jnp.float32)
        _s = jax.random.randint(jax.random.fold_in(_gk, 2), (12500,), 0, 50000, jnp.int32)
        _d = jax.random.randint(jax.random.fold_in(_gk, 3), (12500,), 0, 50000, jnp.int32)
        _loop = jnp.arange(50000, dtype=jnp.int32)
        src = jnp.concatenate([_s, _d, _loop])
        dst = jnp.concatenate([_d, _s, _loop])
        _o = jnp.argsort(dst, stable=True)
        src = src[_o]
        dst = dst[_o]
        return (x, src, dst)
    x, src, dst = _rec_inputs()

    def _L0_gnn_setup():
        import jax, jax.numpy as jnp
        import numpy as np
        N_NODES = 100000
        F_DIM = 256
        NNZ = 25000

        def _prelu(x, a):
            return jnp.where(x >= 0, x, a * x)

        def _hconv(x, W, b, src, dst, n):
            xt = x @ W
            ones = jnp.ones(src.shape, xt.dtype)
            D = jax.ops.segment_sum(ones, src, num_segments=n)
            B = jax.ops.segment_sum(ones, dst, num_segments=n)
            Dinv = jnp.where(D > 0, 1.0 / D, 0.0)
            Binv = jnp.where(B > 0, 1.0 / B, 0.0)
            m = jax.ops.segment_sum(xt[src], dst, num_segments=n) * Binv[:, None]
            out = jax.ops.segment_sum(m[dst], src, num_segments=n) * Dinv[:, None]
            return out + b
        key = jax.random.key(seed)
        k0, k1, k2, k3 = jax.random.split(key, 4)
        x = jax.random.normal(k0, (N_NODES, F_DIM), dtype=jnp.float32)
        edge_index = jax.random.randint(k1, (2, NNZ), 0, N_NODES, dtype=jnp.int32)
        scale = (2.0 / F_DIM) ** 0.5
        W1 = jax.random.normal(k2, (F_DIM, F_DIM), dtype=jnp.float32) * scale
        W2 = jax.random.normal(k3, (F_DIM, F_DIM), dtype=jnp.float32) * scale
        b1 = jnp.zeros((F_DIM,), jnp.float32)
        b2 = jnp.zeros((F_DIM,), jnp.float32)
        a = jnp.full((1,), 0.25, jnp.float32)
        return {'x': x, 'edge_index': edge_index, 'W1': W1, 'b1': b1, 'W2': W2, 'b2': b2, 'a': a}
    _L0_gnn_all = _L0_gnn_setup()
    _L0_gnn_in = {k: v for k, v in _L0_gnn_all.items() if k in ('W1', 'b1', 'W2', 'b2', 'a')}
    del _L0_gnn_all

    def _L1_gnn_setup():
        import jax, jax.numpy as jnp
        import numpy as np
        N_NODES = 20000
        N_EDGES = 10000
        D_FEAT = 256
        N_HEADS = 8
        HEAD_DIM = 32
        key = jax.random.key(seed)
        ks = jax.random.split(key, 8)
        nodes = jax.random.normal(ks[0], (N_NODES, D_FEAT), dtype=jnp.float32)
        senders = jax.random.randint(ks[1], (N_EDGES,), 0, N_NODES, dtype=jnp.int32)
        receivers = jax.random.randint(ks[2], (N_EDGES,), 0, N_NODES, dtype=jnp.int32)
        W_s = jax.random.normal(ks[3], (D_FEAT, N_HEADS, HEAD_DIM), dtype=jnp.float32) * 0.05
        b_s = jnp.zeros((N_HEADS, HEAD_DIM), dtype=jnp.float32)
        W_r = jax.random.normal(ks[4], (D_FEAT, N_HEADS, HEAD_DIM), dtype=jnp.float32) * 0.05
        b_r = jnp.zeros((N_HEADS, HEAD_DIM), dtype=jnp.float32)
        a_w = jax.random.normal(ks[5], (HEAD_DIM,), dtype=jnp.float32) * 0.05
        a_b = jnp.zeros((1,), dtype=jnp.float32)
        return {'nodes': nodes, 'senders': senders, 'receivers': receivers, 'W_s': W_s, 'b_s': b_s, 'W_r': W_r, 'b_r': b_r, 'a_w': a_w, 'a_b': a_b}
    _L1_gnn_all = _L1_gnn_setup()
    _L1_gnn_in = {k: v for k, v in _L1_gnn_all.items() if k in ('W_s', 'b_s', 'W_r', 'b_r', 'a_w', 'a_b')}
    del _L1_gnn_all

    def _L2_gnn_setup():
        import jax, jax.numpy as jnp
        import numpy as np
        N, IN, H, C, OUT = (50000, 256, 4, 32, 256)
        E = 12500
        NEG_SLOPE = 0.2

        def _gat_project(x, edge_index, W, att_src, att_dst, bias, Wp, bp):
            n = x.shape[0]
            h_, c_ = att_src.shape
            loops = jnp.arange(n, dtype=edge_index.dtype)
            src = jnp.concatenate([edge_index[0], loops])
            dst = jnp.concatenate([edge_index[1], loops])
            h = (x @ W).reshape(n, h_, c_)
            a_src = jnp.einsum('nhc,hc->nh', h, att_src)
            a_dst = jnp.einsum('nhc,hc->nh', h, att_dst)
            e = jax.nn.leaky_relu(a_src[src] + a_dst[dst], NEG_SLOPE)
            m = jax.ops.segment_max(e, dst, num_segments=n)
            e = jnp.exp(e - m[dst])
            denom = jax.ops.segment_sum(e, dst, num_segments=n)
            alpha = e / (denom[dst] + 1e-16)
            msg = h[src] * alpha[:, :, None]
            out = jax.ops.segment_sum(msg, dst, num_segments=n)
            out = out.reshape(n, h_ * c_) + bias
            return out @ Wp + bp
        key = jax.random.key(seed)
        ks = jax.random.split(key, 8)
        x = jax.random.normal(ks[0], (N, IN), dtype=jnp.float32)
        edge_index = jax.random.randint(ks[1], (2, E), 0, N, dtype=jnp.int64)
        s = 1.0 / np.sqrt(IN)
        W = jax.random.uniform(ks[2], (IN, H * C), minval=-s, maxval=s, dtype=jnp.float32)
        att_src = jax.random.normal(ks[3], (H, C), dtype=jnp.float32) * s
        att_dst = jax.random.normal(ks[4], (H, C), dtype=jnp.float32) * s
        bias = jnp.zeros((H * C,), dtype=jnp.float32)
        sp = 1.0 / np.sqrt(H * C)
        Wp = jax.random.uniform(ks[5], (H * C, OUT), minval=-sp, maxval=sp, dtype=jnp.float32)
        bp = jax.random.uniform(ks[6], (OUT,), minval=-sp, maxval=sp, dtype=jnp.float32)
        return {'x': x, 'edge_index': edge_index, 'W': W, 'att_src': att_src, 'att_dst': att_dst, 'bias': bias, 'Wp': Wp, 'bp': bp}
    _L2_gnn_all = _L2_gnn_setup()
    _L2_gnn_in = {k: v for k, v in _L2_gnn_all.items() if k in ('W', 'att_src', 'att_dst', 'bias', 'Wp', 'bp')}
    del _L2_gnn_all

    def _L3_gnn_setup():
        import jax, jax.numpy as jnp
        import numpy as np
        HEADS = 4
        OUT_CH = 64
        NEG_SLOPE = 0.2
        key = jax.random.key(seed)
        k1, k2, k3, k4, k5 = jax.random.split(key, 5)
        N, E, IN = (50000, 25000, 256)
        x = jax.random.normal(k1, (N, IN), dtype=jnp.float32)
        edge_index = jax.random.randint(k2, (2, E), 0, N, dtype=jnp.int32)
        W = jax.random.normal(k3, (IN, HEADS * OUT_CH), dtype=jnp.float32) * (1.0 / np.sqrt(IN))
        att_src = jax.random.normal(k4, (HEADS, OUT_CH), dtype=jnp.float32) * 0.1
        att_dst = jax.random.normal(k5, (HEADS, OUT_CH), dtype=jnp.float32) * 0.1
        bias = jnp.zeros((HEADS * OUT_CH,), dtype=jnp.float32)
        return {'x': x, 'edge_index': edge_index, 'W': W, 'att_src': att_src, 'att_dst': att_dst, 'bias': bias}
    _L3_gnn_all = _L3_gnn_setup()
    _L3_gnn_in = {k: v for k, v in _L3_gnn_all.items() if k in ('W', 'att_src', 'att_dst', 'bias')}
    del _L3_gnn_all
    return {'x': x, 'src': src, 'dst': dst, 'L0_gnn_W1': _L0_gnn_in['W1'], 'L0_gnn_b1': _L0_gnn_in['b1'], 'L0_gnn_W2': _L0_gnn_in['W2'], 'L0_gnn_b2': _L0_gnn_in['b2'], 'L0_gnn_a': _L0_gnn_in['a'], 'L1_gnn_W_s': _L1_gnn_in['W_s'], 'L1_gnn_b_s': _L1_gnn_in['b_s'], 'L1_gnn_W_r': _L1_gnn_in['W_r'], 'L1_gnn_b_r': _L1_gnn_in['b_r'], 'L1_gnn_a_w': _L1_gnn_in['a_w'], 'L1_gnn_a_b': _L1_gnn_in['a_b'], 'L2_gnn_W': _L2_gnn_in['W'], 'L2_gnn_att_src': _L2_gnn_in['att_src'], 'L2_gnn_att_dst': _L2_gnn_in['att_dst'], 'L2_gnn_bias': _L2_gnn_in['bias'], 'L2_gnn_Wp': _L2_gnn_in['Wp'], 'L2_gnn_bp': _L2_gnn_in['bp'], 'L3_gnn_W': _L3_gnn_in['W'], 'L3_gnn_att_src': _L3_gnn_in['att_src'], 'L3_gnn_att_dst': _L3_gnn_in['att_dst'], 'L3_gnn_bias': _L3_gnn_in['bias']}

def reference(x, src, dst, L0_gnn_W1, L0_gnn_b1, L0_gnn_W2, L0_gnn_b2, L0_gnn_a, L1_gnn_W_s, L1_gnn_b_s, L1_gnn_W_r, L1_gnn_b_r, L1_gnn_a_w, L1_gnn_a_b, L2_gnn_W, L2_gnn_att_src, L2_gnn_att_dst, L2_gnn_bias, L2_gnn_Wp, L2_gnn_bp, L3_gnn_W, L3_gnn_att_src, L3_gnn_att_dst, L3_gnn_bias):
    import jax
    import jax.numpy as jnp

    def _L0_gnn_ref(x, edge_index, W1, b1, W2, b2, a):
        import jax, jax.numpy as jnp
        import numpy as np
        N_NODES = 100000
        F_DIM = 256
        NNZ = 25000

        def _prelu(x, a):
            return jnp.where(x >= 0, x, a * x)

        def _hconv(x, W, b, src, dst, n):
            xt = x @ W
            ones = jnp.ones(src.shape, xt.dtype)
            D = jax.ops.segment_sum(ones, src, num_segments=n)
            B = jax.ops.segment_sum(ones, dst, num_segments=n)
            Dinv = jnp.where(D > 0, 1.0 / D, 0.0)
            Binv = jnp.where(B > 0, 1.0 / B, 0.0)
            m = jax.ops.segment_sum(xt[src], dst, num_segments=n) * Binv[:, None]
            out = jax.ops.segment_sum(m[dst], src, num_segments=n) * Dinv[:, None]
            return out + b
        src, dst = (edge_index[0], edge_index[1])
        n = x.shape[0]
        h = _prelu(_hconv(x, W1, b1, src, dst, n), a)
        h = _hconv(h, W2, b2, src, dst, n) + x
        return _prelu(h, a)

    def _L1_gnn_ref(nodes, senders, receivers, W_s, b_s, W_r, b_r, a_w, a_b):
        import jax, jax.numpy as jnp
        import numpy as np
        N_NODES = 20000
        N_EDGES = 10000
        D_FEAT = 256
        N_HEADS = 8
        HEAD_DIM = 32
        'GATv2 forward (jraph GraphNetwork semantics, globals/edges = None).\n\n            Returns updated node features [N, embed_dim].\n            '
        n = nodes.shape[0]
        sent_proj = jnp.einsum('nd,dhk->nhk', nodes, W_s) + b_s
        recv_proj = jnp.einsum('nd,dhk->nhk', nodes, W_r) + b_r
        msg = sent_proj[senders]
        r = recv_proj[receivers]
        x = jax.nn.leaky_relu(msg + r)
        logits = jnp.einsum('ehk,k->eh', x, a_w) + a_b
        seg_max = jax.ops.segment_max(logits, receivers, num_segments=n)
        e = jnp.exp(logits - seg_max[receivers])
        denom = jax.ops.segment_sum(e, receivers, num_segments=n)
        w = e / denom[receivers]
        weighted = w[..., None] * msg
        agg = jax.ops.segment_sum(weighted, receivers, num_segments=n)
        return agg.reshape(n, -1)

    def _L2_gnn_ref(x, edge_index, W, att_src, att_dst, bias, Wp, bp):
        import jax, jax.numpy as jnp
        import numpy as np
        N, IN, H, C, OUT = (50000, 256, 4, 32, 256)
        E = 12500
        NEG_SLOPE = 0.2

        def _gat_project(x, edge_index, W, att_src, att_dst, bias, Wp, bp):
            n = x.shape[0]
            h_, c_ = att_src.shape
            loops = jnp.arange(n, dtype=edge_index.dtype)
            src = jnp.concatenate([edge_index[0], loops])
            dst = jnp.concatenate([edge_index[1], loops])
            h = (x @ W).reshape(n, h_, c_)
            a_src = jnp.einsum('nhc,hc->nh', h, att_src)
            a_dst = jnp.einsum('nhc,hc->nh', h, att_dst)
            e = jax.nn.leaky_relu(a_src[src] + a_dst[dst], NEG_SLOPE)
            m = jax.ops.segment_max(e, dst, num_segments=n)
            e = jnp.exp(e - m[dst])
            denom = jax.ops.segment_sum(e, dst, num_segments=n)
            alpha = e / (denom[dst] + 1e-16)
            msg = h[src] * alpha[:, :, None]
            out = jax.ops.segment_sum(msg, dst, num_segments=n)
            out = out.reshape(n, h_ * c_) + bias
            return out @ Wp + bp
        return _gat_project(x, edge_index, W, att_src, att_dst, bias, Wp, bp)

    def _L3_gnn_ref(x, edge_index, W, att_src, att_dst, bias):
        import jax, jax.numpy as jnp
        import numpy as np
        HEADS = 4
        OUT_CH = 64
        NEG_SLOPE = 0.2
        N = x.shape[0]
        loop = jnp.arange(N, dtype=edge_index.dtype)
        src = jnp.concatenate([edge_index[0], loop])
        dst = jnp.concatenate([edge_index[1], loop])
        h = (x @ W).reshape(N, HEADS, OUT_CH)
        a_src = jnp.einsum('nhc,hc->nh', h, att_src)
        a_dst = jnp.einsum('nhc,hc->nh', h, att_dst)
        e = a_src[src] + a_dst[dst]
        e = jnp.where(e >= 0, e, NEG_SLOPE * e)
        e_max = jax.ops.segment_max(e, dst, num_segments=N)
        e_exp = jnp.exp(e - e_max[dst])
        denom = jax.ops.segment_sum(e_exp, dst, num_segments=N)
        alpha = e_exp / denom[dst]
        msgs = h[src] * alpha[:, :, None]
        out = jax.ops.segment_sum(msgs, dst, num_segments=N)
        out = out.reshape(N, HEADS * OUT_CH) + bias
        out = jax.nn.relu(out)
        norm = jnp.sqrt(jnp.sum(out * out, axis=-1, keepdims=True))
        out = out / jnp.maximum(norm, 1e-12)
        return out
    edge_index = jnp.stack([src, dst])
    x = _layernorm(x + _L0_gnn_ref(x, edge_index, L0_gnn_W1, L0_gnn_b1, L0_gnn_W2, L0_gnn_b2, L0_gnn_a), axis=-1)
    x = _layernorm(x + _L1_gnn_ref(x, src, dst, L1_gnn_W_s, L1_gnn_b_s, L1_gnn_W_r, L1_gnn_b_r, L1_gnn_a_w, L1_gnn_a_b), axis=-1)
    x = _layernorm(x + _L2_gnn_ref(x, edge_index, L2_gnn_W, L2_gnn_att_src, L2_gnn_att_dst, L2_gnn_bias, L2_gnn_Wp, L2_gnn_bp), axis=-1)
    x = _layernorm(x + _L3_gnn_ref(x, edge_index, L3_gnn_W, L3_gnn_att_src, L3_gnn_att_dst, L3_gnn_bias), axis=-1)
    return x

_drawn_inputs = setup_inputs


def setup_inputs(seed=0):
    import zlib

    import numpy as np

    out = dict(_drawn_inputs(seed))
    spreads = {'L0_gnn_b1': (0.0, 0.1),
     'L0_gnn_b2': (0.0, 0.1),
     'L1_gnn_b_s': (0.0, 0.1),
     'L1_gnn_b_r': (0.0, 2.0),
     'L2_gnn_bias': (0.0, 0.1),
     'L3_gnn_bias': (0.0, 0.8)}
    factors = {'L1_gnn_W_r': 10.831,
     'L2_gnn_att_src': 5.942,
     'L2_gnn_att_dst': 25.329,
     'L3_gnn_att_src': 35.45,
     'L3_gnn_att_dst': 64.0}
    for name, (base, spread) in spreads.items():
        noise = np.random.default_rng([zlib.crc32(name.encode()), seed]).standard_normal(out[name].shape)
        drawn = base * np.exp(spread * noise) if base else spread * noise
        out[name] = jnp.asarray(drawn.astype(out[name].dtype))
    for name, factor in factors.items():
        out[name] = (out[name] * factor).astype(out[name].dtype)
    return out
```

```python
from contextlib import ExitStack

import numpy as np
import concourse.bass as bass
from concourse import mybir

P = 128
TILES = 4
ROWS = TILES * P
F32 = mybir.dt.float32
I32 = mybir.dt.int32
ALU = mybir.AluOpType
ACT = mybir.ActivationFunctionType
AX = mybir.AxisListType
FAR = float(2 ** 20)
BIG = 1.0e30
EPS = 1e-5
STAGE = 8


class Group:

    def __init__(self, half, par):
        self.half, self.par, self.g = half, par, 2 * half + par
        self.static = isinstance(half, int)


class Flow:

    def __init__(self, nc, ctx):
        self.nc, self.ctx, self.sems, self.base = nc, ctx, {}, {}

    def sem(self, name):
        if name not in self.sems:
            self.sems[name] = self.ctx.enter_context(self.nc.semaphore("s_" + name))
            self.base[name] = 0
        return self.sems[name]


class Phase:

    def __init__(self, flow, n_groups):
        self.flow, self.n, self.queue, self.made, self.settled = flow, n_groups, {}, {}, {"gather"}
        self.stores = set()

    def step(self, engine, name, waits, fn, lag=0):
        self.flow.sem(name)
        self.made[name] = 0
        self.queue.setdefault(engine, []).append((lag, name, waits, fn, 0))

    def dma(self, engine, name, waits, fn, count=1, lag=0):
        self.flow.sem(name + "0"), self.flow.sem(name + "1")
        self.made[name] = count
        if engine == "act":
            self.stores.add(name)
        self.queue.setdefault(engine, []).append((lag, name, waits, fn, count))

    def wait(self, eng, q, producer, back):
        k = self.made[producer]
        if k:
            assert back in (0, 2)
            name, count = producer + str(q.par), (q.half + (1 if back == 0 else 0)) * 16 * k
        else:
            name, count = producer, q.g + 1 - back
        if isinstance(count, int) and count <= 0:
            return
        eng.wait_ge(self.flow.sem(name), count + self.flow.base[name])

    def one(self, eng, q, item):
        _, name, waits, fn, count = item
        for producer, back in waits:
            self.wait(eng, q, producer, back)
        if waits and name in self.settled:
            eng.sem_inc(self.flow.sem("passed"), 1)
        if count and name in self.stores and q.static and q.g == self.n - 1:
            s = name + str(1 - q.par)
            uses = (self.n - 2) // 2 + 1
            eng.wait_ge(self.flow.sem(s), self.flow.base[s] + uses * 16 * count)
        if count:
            for d in fn(q):
                d.then_inc(self.flow.sem(name + str(q.par)), 16)
        else:
            fn(q).then_inc(self.flow.sem(name), 1)

    def sweep(self, eng, items):
        last = max(i[0] for i in items)
        lo = (last + 2 + 1) // 2 * 2
        hi = (self.n - 1) // 2 * 2
        lo = min(lo, hi)

        def static(j):
            for i in items:
                g = j - i[0]
                if 0 <= g < self.n:
                    self.one(eng, Group(g // 2, g % 2), i)

        for j in range(lo):
            static(j)
        if hi > lo:
            with eng.Fori(lo // 2, hi // 2) as half:
                for par in range(2):
                    for i in items:
                        k = par - i[0]
                        self.one(eng, Group(half + k // 2 if k // 2 else half, k % 2), i)
        for j in range(hi, self.n + last):
            static(j)

    def run(self, nc):
        with nc.Block() as block:
            marks = {"sp": block.sync, "pool": block.gpsimd, "pe": block.tensor, "dve": block.vector, "act": block.scalar}
            for name, mark in marks.items():
                items = self.queue.get(name, [])
                if not items:
                    continue

                def body(eng, items=items):
                    self.sweep(eng, items)
                    for _, label, _, _, count in items:
                        if count:
                            for par in range(2):
                                uses = (self.n + 1 - par) // 2
                                s = label + str(par)
                                eng.wait_ge(self.flow.sem(s), self.flow.base[s] + uses * 16 * count)
                mark(body)
        for name, count in self.made.items():
            if count:
                for par in range(2):
                    self.flow.base[name + str(par)] += (self.n + 1 - par) // 2 * 16 * count
            else:
                self.flow.base[name] += self.n


def build_program(nc, a, out):
    n, feat = a["x"].shape
    e = a["src"].shape[0]
    links = e - n
    ng = -(-n // ROWS)
    nt = ng * TILES
    last_base = n - ROWS
    kf = feat // P
    V, S, G, T, D = nc.vector, nc.scalar, nc.gpsimd, nc.tensor, nc.sync

    def dram(name, shape, dt=F32):
        return nc.dram_tensor(name, shape, dt, kind="Internal").ap()

    ctx = ExitStack()
    with ctx:
        def sb(name, shape, dt=F32):
            return ctx.enter_context(nc.sbuf_tensor(name, shape, dt))

        flow = Flow(nc, ctx)
        psum = ctx.enter_context(nc.psum_tensor("psum", [P, 4096], F32))

        def bank(first, count):
            return psum[:, first * 512:(first + count) * 512]

        link_recs = dram("link_recs", [links, 4])
        slot_dst = dram("slot_dst", [nt, P])
        slot_open = dram("slot_open", [nt, P])
        hop_a = dram("hop_a", [n, feat])
        hop_b = dram("hop_b", [n, feat])
        x1 = dram("x1", [n, feat])
        x2 = dram("x2", [n, feat])
        x3 = dram("x3", [n, feat])
        tab1 = dram("tab1", [n, feat])
        recv1 = dram("recv1", [n, feat])
        heads1, cols1 = a["L1_gnn_W_s"].shape[1:]
        heads2, cols2 = a["L2_gnn_att_src"].shape
        heads3, cols3 = a["L3_gnn_att_src"].shape
        f2, f3 = heads2 * cols2, heads3 * cols3
        w2, w3 = f2 + 2 * heads2, f3 + 2 * heads3
        tab2 = dram("tab2", [n, w2])
        tab3 = dram("tab3", [n, w3])

        ident = sb("ident", [P, P])
        iota_row = sb("iota_row", [P, P])
        iota_col = sb("iota_col", [P, 1])
        ones = sb("ones", [P, P])
        base_row = sb("base_row", [P, nt])
        link_src = sb("link_src", [P, nt], I32)
        link_dst = sb("link_dst", [P, nt])
        link_end = sb("link_end", [P, nt])
        inv_deg = sb("inv_deg", [P, nt])
        no_link = sb("no_link", [P, nt])
        power = sb("power", [P, 2 * TILES])
        neg_slope = sb("neg_slope", [P, 1])

        weights = {}

        def weight(name, shape, src):
            weights[name] = (sb(name, shape), src)
            return weights[name][0]

        def chunks(w):
            return w.rearrange("(c p) m -> p c m", p=P)

        def spread(row, m):
            return row.rearrange("(o m) -> o m", o=1).to_broadcast([P, m])

        w_l0a = weight("w_l0a", [P, kf, feat], chunks(a["L0_gnn_W1"]))
        w_l0b = weight("w_l0b", [P, kf, feat], chunks(a["L0_gnn_W2"]))
        w_snd = weight("w_snd", [P, kf, feat], chunks(a["L1_gnn_W_s"].rearrange("d h k -> d (h k)")))
        w_rcv = weight("w_rcv", [P, kf, feat], chunks(a["L1_gnn_W_r"].rearrange("d h k -> d (h k)")))
        w_g2 = weight("w_g2", [P, kf, f2], chunks(a["L2_gnn_W"]))
        w_p2 = weight("w_p2", [P, feat], a["L2_gnn_Wp"])
        w_g3 = weight("w_g3", [P, kf, f3], chunks(a["L3_gnn_W"]))
        b_l0a = weight("b_l0a", [P, feat], spread(a["L0_gnn_b1"], feat))
        b_l0b = weight("b_l0b", [P, feat], spread(a["L0_gnn_b2"], feat))
        b_snd = weight("b_snd", [P, feat], spread(a["L1_gnn_b_s"].rearrange("h k -> (h k)"), feat))
        b_rcv = weight("b_rcv", [P, feat], spread(a["L1_gnn_b_r"].rearrange("h k -> (h k)"), feat))
        a_w = weight("a_w", [P, cols1], spread(a["L1_gnn_a_w"], cols1))
        a_b = weight("a_b", [P, 1], spread(a["L1_gnn_a_b"], 1))
        b_g2 = weight("b_g2", [P, f2], spread(a["L2_gnn_bias"], f2))
        b_p2 = weight("b_p2", [P, feat], spread(a["L2_gnn_bp"], feat))
        b_g3 = weight("b_g3", [P, f3], spread(a["L3_gnn_bias"], f3))
        slope = weight("slope", [P, 1], spread(a["L0_gnn_a"], 1))
        att2 = weight("att2", [P, 2, f2], None)
        att3 = weight("att3", [P, 2, f3], None)
        w_a2 = sb("w_a2", [P, kf, 2, heads2])
        w_a3 = sb("w_a3", [P, kf, 2, heads3])
        att_tmp = sb("att_tmp", [P, max(f2, f3)])

        s_w, s_c = flow.sem("weights"), flow.sem("const")

        step_cols = 2 * STAGE
        raw = -(-e // P)
        ec = -(-raw // step_cols) * step_cols
        tail = e - (P - 1) * raw
        assert 2 < tail <= raw and n >= 2 * ROWS
        with ExitStack() as tmp:
            def tb(name, shape, dt=F32):
                return tmp.enter_context(nc.sbuf_tensor(name, shape, dt))
            src_i = tb("src_i", [P, raw], I32)
            near = [tb(f"dst_i{k}", [P, raw], I32) for k in range(4)]
            nearf = [tb(f"dst_f{k}", [P, raw]) for k in range(4)]
            edge_i = tb("edge_i", [P, raw], I32)
            edge_f = tb("edge_f", [P, raw])
            is_end = tb("is_end", [P, raw])
            recs = tb("recs", [P, ec, 4])
            pos = tb("pos", [P, ec], I32)
            base_i = tb("base_i", [P, nt], I32)
            below = tb("below", [P, 512])
            scratch = tb("scratch", [P, raw])
            first_link = tb("first_link", [P, nt])
            slot_idx = tb("slot_idx", [P, nt], I32)
            recs_t = tb("recs_t", [P, nt, 4])
            row_t = tb("row_t", [P, P])
            open_t = tb("open_t", [P, nt])
            in_tile = tb("in_tile", [P, nt])
            tmp_t = tb("tmp_t", [P, nt])
            pos_stage = tb("pos_stage", [P, 2, STAGE], I32)
            rec_stage = tb("rec_stage", [P, 2, STAGE, 4])
            iota_i = tb("iota_i", [P, P + 1], I32)

            pad_value = [-1, -1, -1, -1]
            s_e, s_pad, s_v = flow.sem("edges"), flow.sem("pad"), flow.sem("setup")
            with nc.Block() as block:
                chain = [0]

                def link(ins):
                    chain[0] += 1
                    ins.then_inc(s_v, 1)
                    V.wait_ge(s_v, chain[0])

                @block.sync
                def _(eng):
                    for handle, src in weights.values():
                        if src is not None:
                            eng.dma_start(handle[:], src).then_inc(s_w, 16)
                    for t, name in ((att2, "L2"), (att3, "L3")):
                        for j, side in enumerate(("src", "dst")):
                            v = a[f"{name}_gnn_att_{side}"].rearrange("h c -> (h c)")
                            eng.dma_start(t[:, j, :], spread(v, v.shape[0])).then_inc(s_w, 16)
                    eng.wait_ge(s_pad, 1)
                    for t, shift, src in [(src_i, 0, a["src"])] + [(near[k], k - 1, a["dst"]) for k in range(4)]:
                        head = max(0, -shift)
                        if head:
                            eng.dma_start(t[0:1, head:raw], src[0:raw - head].rearrange("(o m) -> o m", o=1)).then_inc(s_e, 16)
                            eng.dma_start(t[1:P - 1, :], src[raw - head:(P - 1) * raw - head].rearrange("(p m) -> p m", m=raw)).then_inc(s_e, 16)
                        else:
                            eng.dma_start(t[0:P - 1, :], src[shift:(P - 1) * raw + shift].rearrange("(p m) -> p m", m=raw)).then_inc(s_e, 16)
                        got = min(tail - shift, raw) if shift >= 0 else tail
                        eng.dma_start(t[P - 1:P, 0:got], src[(P - 1) * raw + shift:(P - 1) * raw + shift + got].rearrange("(o m) -> o m", o=1)).then_inc(s_e, 16)
                    eng.wait_ge(s_e, 11 * 16)
                    eng.wait_ge(s_w, 16 * (len(weights) - 2 + 4))

                @block.gpsimd
                def _(eng):
                    for k in range(4):
                        eng.memset(near[k][:], pad_value[k])
                    eng.memset(src_i[:], 0).then_inc(s_pad, 1)
                    eng.memset(ident[:], 0.0)
                    eng.memset(ones[:], 1.0)
                    eng.memset(recs[:], 0.0)
                    eng.memset(pos[:], int(FAR))
                    eng.memset(power[:, 0:TILES], -0.5)
                    eng.memset(power[:, TILES:2 * TILES], 0.5)
                    eng.memset(below[:], 0.0)
                    eng.memset(recs_t[:], -FAR).then_inc(s_pad, 1)
                    eng.iota(edge_i[:], [[1, raw]], base=0, channel_multiplier=raw)
                    full = nt - TILES
                    eng.iota(base_i[:, 0:full], [[P, full]], base=0, channel_multiplier=0)
                    eng.iota(base_i[:, full:nt], [[P, TILES]], base=last_base, channel_multiplier=0)
                    eng.iota(iota_i[:, 0:P], [[1, P]], base=0, channel_multiplier=0)
                    eng.iota(iota_i[:, P:P + 1], [[0, 1]], base=0, channel_multiplier=1).then_inc(s_c, 1)
                    eng.wait_ge(s_pad, 2)
                    eng.affine_select(out=ident[:], in_=ident[:], compare_op=ALU.not_equal, fill=1.0, base=0,
                                      pattern=[[-1, P]], channel_multiplier=1).then_inc(s_c, 1)

                @block.vector
                def _(eng):
                    eng.wait_ge(s_c, 2)
                    V.tensor_copy(iota_row[:], iota_i[:, 0:P])
                    V.tensor_copy(iota_col[:], iota_i[:, P:P + 1])
                    V.tensor_copy(base_row[:], base_i[:])
                    V.tensor_copy(edge_f[:], edge_i[:])
                    eng.wait_ge(s_e, 11 * 16)
                    for k in range(4):
                        V.tensor_copy(nearf[k][:], near[k][:])
                    link(V.tensor_copy(recs[:, 0:raw, 0], src_i[:]))
                    before, here, after, after2 = (t[:] for t in nearf)
                    V.tensor_copy(recs[:, 0:raw, 1], here)
                    V.tensor_tensor(is_end[:], here, after, ALU.not_equal)
                    V.tensor_tensor(edge_f[:], edge_f[:], here, ALU.subtract)
                    V.tensor_tensor(scratch[:], after, after2, ALU.is_equal)
                    link(V.tensor_tensor(recs[:, 0:raw, 3], before, here, ALU.not_equal))
                    link(V.tensor_scalar(scratch[:], scratch[:], -FAR, None, ALU.mult))
                    link(V.tensor_tensor(recs[:, 0:raw, 2], scratch[:], here, ALU.add))
                    link(V.scalar_tensor_tensor(scratch[:], is_end[:], FAR, edge_f[:], ALU.mult, ALU.add))
                    link(V.tensor_copy(pos[:, 0:raw], scratch[:]))
                    eng.wait_ge(s_w, 16 * (len(weights) - 2 + 4))
                    link(V.tensor_scalar(neg_slope[:], slope[:], -1.0, None, ALU.mult))
                    for w, att, wa, heads, width in ((w_g2, att2, w_a2, heads2, f2), (w_g3, att3, w_a3, heads3, f3)):
                        for c in range(kf):
                            for j in range(2):
                                link(V.tensor_tensor(att_tmp[:, 0:width], w[:, c, :], att[:, j, :], ALU.mult))
                                link(V.tensor_reduce(wa[:, c, j, :], att_tmp[:, 0:width].rearrange("p (h c) -> p h c", h=heads),
                                                     AX.X, ALU.add))

            rounds = ec // step_cols
            counts = -(-nt // rounds)
            assert counts * rounds <= 512 and nt <= 512
            s_cnt = flow.sem("count")
            s_stage, s_sent = flow.sem("stage"), [flow.sem("sent0"), flow.sem("sent1")]
            thr = tb("thr", [P, counts * rounds])
            with nc.Block() as block:
                @block.vector
                def _(eng):
                    V.memset(thr[:], 0.0).then_inc(s_pad, 1)
                    eng.wait_ge(s_pad, 3)
                    V.tensor_copy(thr[:, 0:nt], base_row[:]).then_inc(s_pad, 1)
                    eng.wait_ge(s_pad, 4)
                    def one_round(r, first):
                        for half in range(2):
                            if not first:
                                eng.wait_ge(s_sent[half], r * (16 * STAGE))
                            c0 = bass.ds(r * step_cols + half * STAGE, STAGE)
                            V.tensor_copy(pos_stage[:, half, :], pos[:, c0])
                            V.tensor_copy(rec_stage[:, half, :, :], recs[:, c0, :]).then_inc(s_stage, 1)
                        for k in range(counts):
                            t = bass.ds(r * counts + k, 1)
                            V.tensor_scalar(scratch[:], nearf[1][:], thr[:, t], 0.0, ALU.is_lt, ALU.add,
                                            accum_out=below[:, t]).then_inc(s_cnt, 1)
                            eng.wait_ge(s_cnt, r * counts + k + 1)

                    one_round(0, True)
                    with eng.Fori(1, rounds) as r:
                        one_round(r, False)

                @block.gpsimd
                def _(eng):
                    with eng.Fori(0, rounds) as r:
                        for half in range(2):
                            eng.wait_ge(s_stage, r * 2 + half + 1)
                            eng.sem_inc(flow.sem("passed"), 1)
                            for k in range(STAGE):
                                eng.indirect_dma_start(
                                    out=link_recs, out_offset=bass.IndirectOffsetOnAxis(ap=pos_stage[:, half, k:k + 1], axis=0),
                                    in_=rec_stage[:, half, k, :], in_offset=None,
                                    bounds_check=links - 1, oob_is_err=False).then_inc(s_sent[half], 16)
                    for half in range(2):
                        eng.wait_ge(s_sent[half], rounds * 16 * STAGE)

            s_q, s_got = flow.sem("first"), [flow.sem("got0"), flow.sem("got1")]
            s_back = flow.sem("back")
            pads = P * raw - e
            full_rounds = nt // step_cols
            extra = -(-(nt - full_rounds * step_cols) // STAGE)
            got = tb("got", [P, 2, STAGE, 4])
            with nc.Block() as block:
                @block.tensor
                def _(eng):
                    T.matmul(bank(0, 1)[:, 0:nt], ones[:], below[:, 0:nt], start=True, stop=True).then_inc(s_q, 1)

                @block.vector
                def _(eng):
                    link(V.memset(got[:], -FAR))
                    eng.wait_ge(s_q, 1)
                    link(V.tensor_tensor(first_link[:], bank(0, 1)[:, 0:nt], base_row[:], ALU.subtract))
                    link(V.tensor_scalar(first_link[:], first_link[:], iota_col[:, 0:1], float(-pads), ALU.add, ALU.add))
                    V.tensor_copy(slot_idx[:], first_link[:]).then_inc(s_q, 1)
                    eng.wait_ge(s_q, 2)

                    def stage(b, half):
                        V.tensor_copy(pos_stage[:, half, :], slot_idx[:, bass.ds(b, STAGE)]).then_inc(s_stage, 1)

                    def take(b, half, r):
                        eng.wait_ge(s_got[half], (r + 1) * (16 * STAGE))
                        V.tensor_copy(recs_t[:, bass.ds(b, STAGE), :], got[:, half, :, :]).then_inc(s_back, 1)

                    with eng.Fori(0, full_rounds) as r:
                        for half in range(2):
                            stage(r * step_cols + half * STAGE, half)
                        for half in range(2):
                            take(r * step_cols + half * STAGE, half, r)
                    for half in range(extra):
                        b = min(full_rounds * step_cols + half * STAGE, nt - STAGE)
                        stage(b, half)
                        take(b, half, full_rounds)
                    eng.wait_ge(s_back, 2 * full_rounds + extra)
                    V.tensor_tensor(link_end[:], recs_t[:, :, 2], base_row[:], ALU.subtract)
                    V.tensor_scalar(open_t[:], recs_t[:, :, 3], -BIG, None, ALU.mult)
                    link(V.tensor_tensor(link_dst[:], recs_t[:, :, 1], base_row[:], ALU.subtract))
                    V.tensor_scalar(in_tile[:], link_dst[:], -0.5, None, ALU.is_gt)
                    link(V.tensor_scalar(tmp_t[:], link_dst[:], P - 0.5, None, ALU.is_lt))
                    link(V.tensor_tensor(in_tile[:], in_tile[:], tmp_t[:], ALU.mult))
                    link(V.tensor_scalar(tmp_t[:], in_tile[:], -FAR, FAR, ALU.mult, ALU.add))
                    link(V.tensor_tensor(tmp_t[:], tmp_t[:], recs_t[:, :, 0], ALU.add))
                    V.tensor_scalar(tmp_t[:], tmp_t[:], 0.0, None, ALU.max).then_inc(s_q, 1)
                    eng.wait_ge(s_q, 3)
                    V.tensor_copy(link_src[:], tmp_t[:]).then_inc(s_q, 1)

                @block.gpsimd
                def _(eng):
                    def fetch(half, seq):
                        eng.wait_ge(s_stage, 2 * rounds + seq + 1)
                        eng.sem_inc(flow.sem("passed"), 1)
                        for k in range(STAGE):
                            eng.indirect_dma_start(
                                out=got[:, half, k, :], out_offset=None, in_=link_recs,
                                in_offset=bass.IndirectOffsetOnAxis(ap=pos_stage[:, half, k:k + 1], axis=0),
                                bounds_check=links - 1, oob_is_err=False).then_inc(s_got[half], 16)
                    eng.wait_ge(s_q, 2)
                    with eng.Fori(0, full_rounds) as r:
                        for half in range(2):
                            fetch(half, r * 2 + half)
                    for x in range(extra):
                        fetch(x, full_rounds * 2 + x)
                    for half in range(2):
                        eng.wait_ge(s_got[half], (full_rounds + (1 if half < extra else 0)) * 16 * STAGE)

            nb = -(-nt // P)
            bt = nt // nb if nt % nb == 0 else None
            assert bt is not None
            s_tr, s_tc, s_ts = flow.sem("row_tr"), flow.sem("row_cp"), flow.sem("row_st")
            with nc.Block() as block:
                @block.tensor
                def _(eng):
                    for i in range(2 * nb):
                        t = (link_dst, open_t)[i // nb]
                        b = i % nb
                        eng.wait_ge(s_tc, i)
                        T.transpose(bank(0, 1)[0:bt, 0:P], t[:, b * bt:(b + 1) * bt], ident[:]).then_inc(s_tr, 1)

                @block.vector
                def _(eng):
                    for i in range(2 * nb):
                        eng.wait_ge(s_tr, i + 1)
                        eng.wait_ge(s_ts, 16 * i)
                        V.tensor_copy(row_t[0:bt, :], bank(0, 1)[0:bt, 0:P]).then_inc(s_tc, 1)

                @block.sync
                def _(eng):
                    for i in range(2 * nb):
                        d = (slot_dst, slot_open)[i // nb]
                        b = i % nb
                        eng.wait_ge(s_tc, i + 1)
                        eng.dma_start(d[b * bt:(b + 1) * bt, :], row_t[0:bt, :]).then_inc(s_ts, 16)
                    eng.wait_ge(s_ts, 16 * 2 * nb)

        wide = max(feat, w2, w3)
        own = sb("own", [P, 2, TILES, feat])
        own_x = sb("own_x", [P, 2, TILES, feat])
        own_r = sb("own_r", [P, 2, TILES, feat])
        own_t = sb("own_t", [P, 2, TILES * wide])
        got_rows = sb("got_rows", [P, 2, TILES * wide])
        idx = sb("idx", [P, 2, TILES], I32)
        sel = sb("sel", [P, 2, TILES, P])
        sel_end = sb("sel_end", [P, 2, TILES, P])
        sel_t = sb("sel_t", [P, 2, TILES, P])
        dst_rows = sb("dst_rows", [P, 2, TILES * P])
        opens = sb("opens", [TILES * heads1, 2, P])
        mean_row = sb("mean_row", [P, 2, TILES, feat])
        xt = sb("xt", [P, TILES, kf, P])
        t0 = sb("t0", [P, TILES, feat])
        t1 = sb("t1", [P, TILES, feat])
        t2 = sb("t2", [P, TILES, feat])
        t3 = sb("t3", [P, TILES, feat])
        z = sb("z", [P, 2 * TILES, feat])
        res = sb("res", [P, 2, TILES, feat])
        res_b = sb("res_b", [P, 2, TILES, feat])
        tab_o = sb("tab_o", [P, 2, TILES * wide])
        stats = sb("stats", [P, TILES, 6])
        moments = sb("moments", [P, TILES, 5])
        var_eps = sb("var_eps", [P, TILES])
        rstd = sb("rstd", [P, TILES])
        shift = sb("shift", [P, TILES])
        deg = sb("deg", [P, TILES])
        sq = sb("sq", [P, TILES])
        scanned = sb("scanned", [P, P])

        s_init = flow.sem("init")
        with nc.Block() as block:
            @block.gpsimd
            def _(eng):
                eng.memset(got_rows[:], 0.0).then_inc(s_init, 1)
                eng.memset(scanned[:], 0.0).then_inc(s_init, 1)
                eng.wait_ge(s_init, 2)

        def rows(t, q):
            r0 = min(q.g * ROWS, last_base) if q.static else None
            sl = slice(r0, r0 + ROWS) if q.static else bass.ds(q.g * ROWS, ROWS)
            return t[sl, :].rearrange("(k p) f -> p k f", p=P)

        def tiles(q, k=None):
            c0, m = (q.g * TILES, TILES) if k is None else (q.g * TILES + k, 1)
            return slice(c0, c0 + m) if q.static else bass.ds(c0, m)

        def split(t, par, width):
            return t[:, par, 0:TILES * width].rearrange("p (k w) -> p k w", k=TILES)

        def fetch_links(ph, table, width, done):
            ph.step("dve", "idx", [(done, 2), ("gather", 2)],
                    lambda q: V.tensor_copy(idx[:, q.par, :], link_src[:, tiles(q)]))
            ph.dma("pool", "gather", [("idx", 0), (done, 2)], lambda q: [
                G.indirect_dma_start(out=got_rows[:, q.par, k * width:(k + 1) * width], out_offset=None, in_=table,
                                     in_offset=bass.IndirectOffsetOnAxis(ap=idx[:, q.par, k:k + 1], axis=0),
                                     bounds_check=n - 1, oob_is_err=False) for k in range(TILES)], count=TILES)
            ph.step("dve", "sel", [(done, 2)], lambda q: V.tensor_tensor(
                sel[:, q.par], iota_row[:].unsqueeze(1).to_broadcast([P, TILES, P]),
                link_dst[:, tiles(q)].unsqueeze(2).to_broadcast([P, TILES, P]), ALU.is_equal))

        def transpose_rows(ph, name, src, ps, after, ps_free, chunks_=kf, xt_free=()):
            def tr(q):
                for k in range(TILES):
                    for c in range(chunks_):
                        o = (k * chunks_ + c) * P
                        i = T.transpose(ps[:, o:o + P], src(q)[:, k, c * P:(c + 1) * P], ident[:])
                return i
            ph.step("pe", name + "_tr", after + ps_free, tr)
            ph.step("dve", name + "_xt", [(name + "_tr", 0)] + list(xt_free), lambda q: V.tensor_copy(
                xt[:].rearrange("p k c f -> p (k c f)")[:, 0:TILES * chunks_ * P], ps[:, 0:TILES * chunks_ * P]))

        def dense(ph, name, w, width, ps, waits, extra=None, chunks_=kf):
            xv = xt[:].rearrange("p k c f -> p (k c f)")

            def mm(q):
                for k in range(TILES):
                    for c in range(chunks_):
                        o = (k * chunks_ + c) * P
                        i = T.matmul(ps[:, k * width:(k + 1) * width], xv[:, o:o + P], w[:, c, :] if chunks_ > 1 else w[:],
                                     start=(c == 0), stop=(c == chunks_ - 1 and extra is None))
                    if extra is not None:
                        i = T.matmul(ps[:, k * width:(k + 1) * width], ident[:], extra(q, k), start=False, stop=True)
                return i
            ph.step("pe", name, waits, mm)

        def layer_norm(ph, src, after, dst, dst_free):
            def st(q):
                for k in range(TILES):
                    i = V.bn_stats(stats[:, k, :], src(q)[:, k, :])
                return i

            def halves(q):
                V.tensor_tensor(moments[:, :, 0], stats[:, :, 1], stats[:, :, 4], ALU.add)
                V.tensor_tensor(moments[:, :, 1], stats[:, :, 1], stats[:, :, 4], ALU.subtract)
                return V.tensor_tensor(moments[:, :, 2], stats[:, :, 2], stats[:, :, 5], ALU.add)

            def parts(q):
                V.tensor_scalar(moments[:, :, 3], moments[:, :, 2], 1.0 / feat, EPS, ALU.mult, ALU.add)
                return V.scalar_tensor_tensor(moments[:, :, 4], moments[:, :, 1], 0.25, moments[:, :, 1], ALU.mult, ALU.mult)

            def ln(q):
                for k in range(TILES):
                    i = S.activation(dst(q)[:, k, :], src(q)[:, k, :], ACT.Identity, bias=shift[:, k:k + 1], scale=rstd[:, k:k + 1])
                return i
            ph.step("dve", "stats", after, st)
            ph.step("dve", "halves", [("stats", 0)], halves)
            ph.step("dve", "parts", [("halves", 0)], parts)
            ph.step("dve", "veps", [("parts", 0)], lambda q: V.tensor_tensor(var_eps[:], moments[:, :, 3], moments[:, :, 4], ALU.add))
            ph.step("pool", "rstd", [("veps", 0), ("ln", 1)], lambda q: G.tensor_tensor(rstd[:], var_eps[:], power[:, 0:TILES], ALU.pow))
            ph.step("dve", "shift", [("rstd", 0)], lambda q: V.scalar_tensor_tensor(
                shift[:], moments[:, :, 0], -0.5, rstd[:], ALU.mult, ALU.mult))
            ph.step("act", "ln", [("shift", 0)] + dst_free, ln)

        def grid(ps, width):
            return ps.rearrange("p (k w) -> p k w", k=TILES)[:, :, 0:width] if width * TILES == ps.shape[1] else \
                ps[:, 0:TILES * width].rearrange("p (k w) -> p k w", k=TILES)

        def bc(row, width):
            return row[:, 0:width].unsqueeze(1).to_broadcast([P, TILES, width])

        def hop(table, kind, outs, first=False):
            ph = Phase(flow, ng)
            agg = [bank(0, 2), bank(2, 2)]
            ph.dma("sp", "own", [("agg", 2)], lambda q: [D.dma_start(own[:, q.par], rows(table, q))])
            if kind == "x1":
                ph.dma("sp", "own_x", [("add_x", 2)], lambda q: [D.dma_start(own_x[:, q.par], rows(a["x"], q))])
            fetch_links(ph, table, feat, "agg")

            def sum_links(q):
                g = split(got_rows, q.par, feat)
                for k in range(TILES):
                    o = agg[q.par][:, k * feat:(k + 1) * feat]
                    T.matmul(o, sel[:, q.par, k, :], g[:, k, :], start=True, stop=False)
                    i = T.matmul(o, ident[:], own[:, q.par, k, :], start=False, stop=True)
                    if first:
                        i = T.matmul(bank(4, 1)[:, k:k + 1], sel[:, q.par, k, :], ones[:, 0:1], start=True, stop=True)
                return i
            ph.step("pe", "agg", [("own", 0), ("gather", 0), ("sel", 0), ("mean", 2)] + ([("no_link", 1)] if first else []), sum_links)
            if first:
                ph.step("dve", "deg", [("agg", 0)], lambda q: V.tensor_scalar(deg[:], bank(4, 1)[:, 0:TILES], 1.0, None, ALU.add))
                ph.step("dve", "no_link", [("deg", 0)], lambda q: V.tensor_scalar(
                    no_link[:, tiles(q)], bank(4, 1)[:, 0:TILES], 0.5, -BIG, ALU.is_lt, ALU.mult))
                ph.step("dve", "inv", [("deg", 0)], lambda q: V.reciprocal(inv_deg[:, tiles(q)], deg[:]))

            def mean(q):
                for k in range(TILES):
                    i = S.mul(mean_row[:, q.par, k, :], agg[q.par][:, k * feat:(k + 1) * feat], inv_deg[:, tiles(q, k)])
                return i
            mean_free = ("store", 2) if kind == "hop" else ("up_tr", 2)
            ph.step("act", "mean", [("agg", 0), mean_free] + ([("inv", 0)] if first else []), mean)
            if kind == "hop":
                ph.dma("act", "store", [("mean", 0)], lambda q: [S.dma_start(rows(outs[0], q), mean_row[:, q.par])])
                ph.run(nc)
                return
            w, b = (w_l0a, b_l0a) if kind == "h1" else (w_l0b, b_l0b)
            tp, dn = bank(4, 2), bank(6, 2)
            mm_free = [("snd_mm", 1)] if kind == "x1" else []
            transpose_rows(ph, "up", lambda q: mean_row[:, q.par], tp, [("mean", 0)], [("up_xt", 1)] + ([("x1_xt", 1)] if kind == "x1" else []),
                           xt_free=[("up_mm", 1)] + ([("rcv_mm", 1)] if kind == "x1" else []))
            dense(ph, "up_mm", w, feat, dn, [("up_xt", 0), ("biased", 1)] + ([("rcv", 1)] if kind == "x1" else []))
            if kind == "x1":
                ph.step("dve", "pre_b", [("up_mm", 0)], lambda q: V.tensor_tensor(t0[:], grid(dn, feat), bc(b, feat), ALU.add))
                ph.step("dve", "biased", [("pre_b", 0), ("own_x", 0), ("neg", 1)],
                        lambda q: V.tensor_tensor(t0[:], t0[:], own_x[:, q.par], ALU.add))
            else:
                ph.step("dve", "biased", [("up_mm", 0), ("neg", 1)], lambda q: V.tensor_tensor(t0[:], grid(dn, feat), bc(b, feat), ALU.add))
            ph.step("act", "pos", [("biased", 0), ("prelu", 1)], lambda q: S.activation(t1[:], t0[:], ACT.Relu))
            ph.step("act", "neg", [("biased", 0)], lambda q: S.activation(t2[:], t0[:], ACT.Relu, scale=-1.0))
            if kind == "h1":
                ph.step("dve", "prelu", [("neg", 0), ("store", 2)], lambda q: V.scalar_tensor_tensor(
                    res[:, q.par], t2[:], neg_slope[:, 0:1], t1[:], ALU.mult, ALU.add))
                ph.dma("act", "store", [("prelu", 0)], lambda q: [S.dma_start(rows(outs[0], q), res[:, q.par])], lag=1)
                ph.run(nc)
                return
            ph.step("dve", "prelu", [("neg", 0), ("ln", 1)], lambda q: V.scalar_tensor_tensor(
                t3[:], t2[:], neg_slope[:, 0:1], t1[:], ALU.mult, ALU.add))
            ph.step("dve", "add_x", [("prelu", 0)], lambda q: V.tensor_tensor(t3[:], t3[:], own_x[:, q.par], ALU.add))
            layer_norm(ph, lambda q: t3, [("add_x", 0)], lambda q: res[:, q.par], [("store", 2), ("x1_tr", 2)])
            ph.dma("act", "store", [("ln", 0)], lambda q: [S.dma_start(rows(outs[0], q), res[:, q.par])])
            transpose_rows(ph, "x1", lambda q: res[:, q.par], tp, [("ln", 0)], [("up_xt", 0)], xt_free=[("up_mm", 0)])
            dense(ph, "snd_mm", w_snd, feat, dn, [("x1_xt", 0), ("biased", 0)])
            ph.step("dve", "snd", [("snd_mm", 0), ("snd_st", 2)], lambda q: V.tensor_tensor(split(tab_o, q.par, feat), grid(dn, feat), bc(b_snd, feat), ALU.add))
            dense(ph, "rcv_mm", w_rcv, feat, dn, [("x1_xt", 0), ("snd", 0)])
            ph.step("dve", "rcv", [("rcv_mm", 0), ("rcv_st", 2)], lambda q: V.tensor_tensor(res_b[:, q.par], grid(dn, feat), bc(b_rcv, feat), ALU.add))
            ph.dma("act", "snd_st", [("snd", 0)], lambda q: [S.dma_start(rows(outs[1], q), split(tab_o, q.par, feat))], lag=1)
            ph.dma("act", "rcv_st", [("rcv", 0)], lambda q: [S.dma_start(rows(outs[2], q), res_b[:, q.par])], lag=1)
            ph.run(nc)

        gat_small = {k: sb("g_" + k, [P, TILES, heads1]) for k in
                     ("maxes", "mx", "d_self", "p_self", "d_link", "p_link", "den", "inv", "w_link", "w_self")}
        logits = sb("logits", [P, 2 * TILES, heads1])

        def gat(xin, table, width, heads, cols, loops, finish, v2=False):
            ph = Phase(flow, ng)
            f = heads * cols
            hk = TILES * heads
            pa, pb, dn = bank(0, 2), bank(2, 2), bank(4, 2)
            small = [bank(6, 1), bank(7, 1)]

            def sm(q, i):
                return small[q.par][:, P + i * 32:P + i * 32 + hk].rearrange("p (k h) -> p k h", k=TILES)
            tmp = {k: v[:, :, 0:heads] if heads < heads1 else v[:] for k, v in gat_small.items()}
            le, ls = logits[:, 0:TILES, 0:heads], logits[:, TILES:2 * TILES, 0:heads]
            lflat = sb(f"lflat{width}", [P, TILES * heads])
            ph.dma("sp", "own_t", [("v_self", 2)] + ([] if not v2 else []), lambda q: [D.dma_start(split(own_t, q.par, width), rows(table, q))])
            if v2:
                ph.dma("sp", "own_r", [("z_self", 2), ("spread_r", 2)], lambda q: [D.dma_start(own_r[:, q.par], rows(recv1, q))])

            def slot_rows(t, q):
                c0 = q.g * TILES
                return t[slice(c0, c0 + TILES) if q.static else bass.ds(c0, TILES), :]
            ph.dma("sp", "dst_row", [("sel_t", 2)], lambda q: [D.dma_start(
                dst_rows[:, q.par, :], slot_rows(slot_dst, q).rearrange("(o k) s -> o (k s)", o=1).to_broadcast([P, TILES * P]))])
            ph.dma("sp", "open_row", [("scan", 2)], lambda q: [D.dma_start(
                opens[k * heads:(k + 1) * heads, q.par, :], slot_rows(slot_open, q)[k:k + 1, :].to_broadcast([heads, P])) for k in range(TILES)], count=TILES)
            ph.dma("sp", "own_x", [("x_read", 2)], lambda q: [D.dma_start(own_x[:, q.par], rows(xin, q))])
            fetch_links(ph, table, width, "agg")
            ph.step("dve", "sel_t", [("dst_row", 0), ("agg", 2)], lambda q: V.tensor_scalar(
                sel_t[:, q.par].rearrange("p k s -> p (k s)"), dst_rows[:, q.par, :], iota_col[:, 0:1], None, ALU.is_equal))
            ph.step("dve", "sel_end", [("agg", 2)], lambda q: V.tensor_tensor(
                sel_end[:, q.par], iota_row[:].unsqueeze(1).to_broadcast([P, TILES, P]),
                link_end[:, tiles(q)].unsqueeze(2).to_broadcast([P, TILES, P]), ALU.is_equal))

            def each(out, lhs, rhs):
                def go(q):
                    for k in range(TILES):
                        i = T.matmul(out(q)[:, k, :], lhs[:, q.par, k, :], rhs(q)[:, k, :], start=True, stop=True)
                    return i
                return go
            if v2:
                ph.step("pe", "spread_r", [("own_r", 0), ("sel_t", 0), ("t_xt", 1), ("z_link", 1)],
                        each(lambda q: grid(pa, feat), sel_t, lambda q: own_r[:, q.par]))
                ph.step("dve", "z_self", [("own_r", 0), ("own_t", 0), ("logit", 1)], lambda q: V.tensor_tensor(
                    z[:, TILES:2 * TILES, :], split(own_t, q.par, feat), own_r[:, q.par], ALU.add))
                ph.step("dve", "z_link", [("spread_r", 0), ("gather", 0)], lambda q: V.tensor_tensor(
                    z[:, 0:TILES, :], grid(pa, feat), split(got_rows, q.par, feat), ALU.add))
                ph.step("dve", "leaky", [("z_link", 0), ("z_self", 0)], lambda q: V.scalar_tensor_tensor(z[:], z[:], 0.01, z[:], ALU.mult, ALU.max))
                ph.step("dve", "z_w", [("leaky", 0)], lambda q: V.tensor_tensor(
                    z[:].rearrange("p k (h c) -> p (k h) c", c=cols), z[:].rearrange("p k (h c) -> p (k h) c", c=cols),
                    a_w[:].unsqueeze(1).to_broadcast([P, 2 * TILES * heads, cols]), ALU.mult))
                ph.step("dve", "z_sum", [("z_w", 0)], lambda q: V.tensor_reduce(
                    logits[:].rearrange("p k h -> p (k h)"), z[:].rearrange("p k (h c) -> p (k h) c", c=cols), AX.X, ALU.add))
                ph.step("dve", "logit", [("z_sum", 0)], lambda q: V.tensor_scalar(
                    logits[:], logits[:], a_b[:, 0:1], None, ALU.add))
            else:
                ph.step("pe", "spread_a", [("own_t", 0), ("sel_t", 0)], each(
                    lambda q: sm(q, 0), sel_t, lambda q: split(own_t, q.par, width)[:, :, f + heads:f + 2 * heads]))
                ph.step("dve", "z_self", [("own_t", 0), ("logit", 1)], lambda q: V.tensor_tensor(
                    ls, split(own_t, q.par, width)[:, :, f:f + heads], split(own_t, q.par, width)[:, :, f + heads:f + 2 * heads], ALU.add))
                ph.step("dve", "z_link", [("spread_a", 0), ("gather", 0)], lambda q: V.tensor_tensor(
                    le, sm(q, 0), split(got_rows, q.par, width)[:, :, f:f + heads], ALU.add))
                lg = logits[:, :, 0:heads]
                ph.step("dve", "logit", [("z_link", 0), ("z_self", 0)], lambda q: V.scalar_tensor_tensor(
                    lg, lg, 0.2, lg, ALU.mult, ALU.max))
            ph.step("dve", "l_flat", [("logit", 0), ("l_tr", 1)], lambda q: V.tensor_copy(lflat[:].rearrange("p (k h) -> p k h", k=TILES), le))
            ph.step("pe", "l_tr", [("l_flat", 0), ("scan", 2)], lambda q: T.transpose(small[q.par][0:hk, 0:P], lflat[:], ident[:]))
            ph.step("dve", "scan", [("l_tr", 0), ("open_row", 0), ("s_tr", 1)], lambda q: V.tensor_tensor_scan(
                scanned[0:hk, :], opens[0:hk, q.par, :], small[q.par][0:hk, 0:P], -BIG, ALU.add, ALU.max))
            ph.step("pe", "s_tr", [("scan", 0)], lambda q: T.matmul(small[q.par][:, P + 32:P + 32 + hk], scanned[:], ident[:, 0:hk], start=True, stop=True))
            ph.step("act", "s_back", [("s_tr", 0), ("seg_max", 1)], lambda q: S.copy(tmp["maxes"], sm(q, 1)))
            ph.step("pe", "seg_max", [("s_back", 0), ("sel_end", 0)], each(lambda q: sm(q, 2), sel_end, lambda q: tmp["maxes"]))
            ph.step("dve", "mx0", [("seg_max", 0), ("spread_m", 1)], lambda q: V.tensor_tensor(
                tmp["mx"], sm(q, 2), no_link[:, tiles(q)].unsqueeze(2).to_broadcast([P, TILES, heads]), ALU.add))
            ph.step("dve", "mx", [("mx0", 0)], lambda q: V.tensor_tensor(tmp["mx"], tmp["mx"], ls, ALU.max))
            ph.step("pe", "spread_m", [("mx", 0)], each(lambda q: sm(q, 3), sel_t, lambda q: tmp["mx"]))
            ph.step("dve", "d_self", [("mx", 0), ("p_self", 1)], lambda q: V.tensor_tensor(tmp["d_self"], ls, tmp["mx"], ALU.subtract))
            ph.step("act", "p_self", [("d_self", 0), ("w_self", 1)], lambda q: S.activation(tmp["p_self"], tmp["d_self"], ACT.Exp))
            ph.step("dve", "d_link0", [("spread_m", 0), ("p_link", 1)], lambda q: V.tensor_tensor(tmp["d_link"], le, sm(q, 3), ALU.subtract))
            ph.step("dve", "d_link", [("d_link0", 0)], lambda q: V.tensor_scalar(tmp["d_link"], tmp["d_link"], 0.0, None, ALU.min))
            ph.step("act", "p_link", [("d_link", 0), ("w_link", 1)], lambda q: S.activation(tmp["p_link"], tmp["d_link"], ACT.Exp))
            ph.step("pe", "sum_p", [("p_link", 0)], each(lambda q: sm(q, 4), sel, lambda q: tmp["p_link"]))
            ph.step("dve", "den0", [("sum_p", 0), ("p_self", 0)], lambda q: V.scalar_tensor_tensor(
                tmp["den"], tmp["p_self"], float(loops), sm(q, 4), ALU.mult, ALU.add))
            ph.step("dve", "den", [("den0", 0)], lambda q: V.tensor_scalar(tmp["den"], tmp["den"], 1e-16 if finish == "project" else 0.0, None, ALU.add))
            ph.step("dve", "inv", [("den", 0), ("spread_i", 1)], lambda q: V.reciprocal(tmp["inv"], tmp["den"]))
            ph.step("pe", "spread_i", [("inv", 0)], each(lambda q: sm(q, 5), sel_t, lambda q: tmp["inv"]))
            ph.step("dve", "w_self", [("inv", 0)], lambda q: V.scalar_tensor_tensor(
                tmp["w_self"], tmp["p_self"], float(loops), tmp["inv"], ALU.mult, ALU.mult))
            ph.step("dve", "w_link", [("spread_i", 0)], lambda q: V.tensor_tensor(tmp["w_link"], tmp["p_link"], sm(q, 5), ALU.mult))
            zl = z[:, 0:TILES, 0:f]
            zs = z[:, TILES:2 * TILES, 0:f]

            def heads4(v):
                return v.rearrange("p k (h c) -> p k h c", c=cols)
            ph.step("dve", "v_self", [("w_self", 0), ("agg", 1)], lambda q: V.tensor_tensor(
                heads4(zs), heads4(split(own_t, q.par, width)[:, :, 0:f]),
                tmp["w_self"].unsqueeze(3).to_broadcast([P, TILES, heads, cols]), ALU.mult))
            ph.step("dve", "v_link", [("w_link", 0), ("agg", 1)], lambda q: V.tensor_tensor(
                heads4(zl), heads4(split(got_rows, q.par, width)[:, :, 0:f]),
                tmp["w_link"].unsqueeze(3).to_broadcast([P, TILES, heads, cols]), ALU.mult))

            def agg(q):
                for k in range(TILES):
                    o = pb[:, k * f:(k + 1) * f]
                    T.matmul(o, sel[:, q.par, k, :], zl[:, k, :], start=True, stop=False)
                    i = T.matmul(o, ident[:], zs[:, k, :], start=False, stop=not v2)
                    if v2:
                        i = T.matmul(o, ident[:], own_x[:, q.par, k, :], start=False, stop=True)
                return i
            ph.step("pe", "agg", [("v_self", 0), ("v_link", 0)] + ([("own_x", 0), ("ln", 1)] if v2 else [("out_b", 1)]), agg)
            pbg = grid(pb, f)

            def table_out(nxt_w, nxt_wa, nf, nheads, nwidth, dst, xsrc):
                transpose_rows(ph, "t", xsrc, pa, [("ln", 0)], [("t_xt", 1)] + ([("z_link", 0)] if v2 else [("o_xt", 0)]),
                               xt_free=[("t_mm", 1)] + ([] if v2 else [("o_mm", 0)]))
                dense(ph, "t_mm0", nxt_w, nf, dn, [("t_xt", 0), ("t_h", 1)] + ([] if v2 else [("out", 0)]))
                att = lambda q: small[q.par][:, P + 192:P + 192 + TILES * 2 * nheads]
                def mm(q):
                    for k in range(TILES):
                        for c in range(kf):
                            i = T.matmul(att(q)[:, k * 2 * nheads:(k + 1) * 2 * nheads], xt[:, k, c, :],
                                         nxt_wa[:, c].rearrange("p j h -> p (j h)"), start=(c == 0), stop=(c == kf - 1))
                    return i
                ph.step("pe", "t_mm", [("t_a", 2)], mm)
                o = lambda q: split(tab_o, q.par, nwidth)
                ph.step("act", "t_h", [("t_mm", 0), ("t_st", 2)], lambda q: S.copy(o(q)[:, :, 0:nf], grid(dn, nf)))
                ph.step("act", "t_a", [("t_mm", 0), ("t_st", 2)], lambda q: S.copy(
                    o(q)[:, :, nf:nwidth], att(q).rearrange("p (k w) -> p k w", k=TILES)))
                ph.dma("act", "t_st", [("t_h", 0), ("t_a", 0)], lambda q: [S.dma_start(rows(dst, q), o(q))])

            if finish == "x2":
                ph.step("dve", "x_read", [("agg", 0)], lambda q: V.tensor_copy(sq[:], deg[:]))
                layer_norm(ph, lambda q: pbg, [("agg", 0)], lambda q: res[:, q.par], [("store", 2), ("t_tr", 2)])
                ph.dma("act", "store", [("ln", 0)], lambda q: [S.dma_start(rows(x2, q), res[:, q.par])])
                table_out(w_g2, w_a2, f2, heads2, w2, tab2, lambda q: res[:, q.par])
            elif finish == "project":
                ph.step("dve", "out_b", [("agg", 0), ("o_tr", 1)], lambda q: V.tensor_tensor(t0[:, :, 0:f], pbg, bc(b_g2, f), ALU.add))
                transpose_rows(ph, "o", lambda q: t0, pa, [("out_b", 0)], [("o_xt", 1), ("t_xt", 1)], chunks_=1, xt_free=[("o_mm", 1), ("t_mm", 1)])
                dense(ph, "o_mm", w_p2, feat, dn, [("o_xt", 0), ("out", 1), ("t_h", 1), ("own_x", 0)],
                      extra=lambda q, k: own_x[:, q.par, k, :], chunks_=1)
                ph.step("dve", "out", [("o_mm", 0), ("ln", 1)], lambda q: V.tensor_tensor(t3[:], grid(dn, feat), bc(b_p2, feat), ALU.add))
                ph.step("dve", "x_read", [("o_mm", 0)], lambda q: V.tensor_copy(sq[:], deg[:]))
                layer_norm(ph, lambda q: t3, [("out", 0)], lambda q: res[:, q.par], [("store", 2), ("t_tr", 2)])
                ph.dma("act", "store", [("ln", 0)], lambda q: [S.dma_start(rows(x3, q), res[:, q.par])])
                table_out(w_g3, w_a3, f3, heads3, w3, tab3, lambda q: res[:, q.par])
            else:
                ph.step("dve", "out_b", [("agg", 0), ("sq", 1)], lambda q: V.tensor_tensor(t0[:], pbg, bc(b_g3, f), ALU.add))
                ph.step("act", "relu", [("out_b", 0), ("x_read", 1)], lambda q: S.activation(t1[:], t0[:], ACT.Relu))

                def square(q):
                    for k in range(TILES):
                        i = S.activation(t2[:, k, :], t1[:, k, :], ACT.Square, accum_out=sq[:, k:k + 1])
                    return i
                ph.step("act", "sq", [("relu", 0), ("norm", 1)], square)
                ph.step("pool", "norm", [("sq", 0), ("norm_c", 1)], lambda q: G.tensor_tensor(deg[:], sq[:], power[:, TILES:2 * TILES], ALU.pow))
                ph.step("dve", "norm_c", [("norm", 0)], lambda q: V.tensor_scalar(var_eps[:], deg[:], 1e-12, None, ALU.max))
                ph.step("dve", "inv_n", [("norm_c", 0)], lambda q: V.reciprocal(shift[:], var_eps[:]))

                def add_x(q):
                    for k in range(TILES):
                        i = V.scalar_tensor_tensor(t3[:, k, :], t1[:, k, :], shift[:, k:k + 1], own_x[:, q.par, k, :], ALU.mult, ALU.add)
                    return i
                ph.step("dve", "x_read", [("inv_n", 0), ("own_x", 0), ("ln", 1)], add_x)
                layer_norm(ph, lambda q: t3, [("x_read", 0)], lambda q: res[:, q.par], [("store", 2)])
                ph.dma("act", "store", [("ln", 0)], lambda q: [S.dma_start(rows(out, q), res[:, q.par])])
            ph.run(nc)

        hop(a["x"], "hop", [hop_a], first=True)
        hop(hop_a, "h1", [hop_b])
        hop(hop_b, "hop", [hop_a])
        hop(hop_a, "x1", [x1, tab1, recv1])
        gat(x1, tab1, feat, heads1, cols1, 1, "x2", v2=True)
        gat(x2, tab2, w2, heads2, cols2, 2, "project")
        gat(x3, tab3, w3, heads3, cols3, 2, "out")


INPUTS = ["x", "src", "dst", "L0_gnn_W1", "L0_gnn_b1", "L0_gnn_W2", "L0_gnn_b2", "L0_gnn_a", "L1_gnn_W_s", "L1_gnn_b_s",
          "L1_gnn_W_r", "L1_gnn_b_r", "L1_gnn_a_w", "L1_gnn_a_b", "L2_gnn_W", "L2_gnn_att_src", "L2_gnn_att_dst",
          "L2_gnn_bias", "L2_gnn_Wp", "L2_gnn_bp", "L3_gnn_W", "L3_gnn_att_src", "L3_gnn_att_dst", "L3_gnn_bias"]


def kernel(**inputs):
    import concourse.bacc as bacc
    from concourse.bass_utils import run_bass_kernel_spmd

    nc = bacc.Bacc("TRN2", target_bir_lowering=False, num_devices=1)
    arrays, args = {}, {}
    for name in INPUTS:
        v = np.ascontiguousarray(inputs[name])
        arrays["in_" + name] = v
        args[name] = nc.dram_tensor("in_" + name, v.shape, mybir.dt.from_np(v.dtype), kind="ExternalInput").ap()
    out = nc.dram_tensor("out", args["x"].shape, F32, kind="ExternalOutput").ap()
    build_program(nc, args, out)
    return run_bass_kernel_spmd(nc, [arrays], core_ids=[0]).results[0]["out"]
```

```python
from contextlib import ExitStack

import numpy as np
import concourse.bass as bass
from concourse import mybir

P = 128
TILES = 4
ROWS = TILES * P
F32 = mybir.dt.float32
I32 = mybir.dt.int32
ALU = mybir.AluOpType
ACT = mybir.ActivationFunctionType
AX = mybir.AxisListType
FAR = float(2 ** 20)
BIG = 1.0e30
EPS = 1e-5
STAGE = 8


RING = 4


class Group:

    def __init__(self, lap, slot):
        self.lap, self.slot, self.par = lap, slot, slot % 2
        self.g = RING * lap + slot
        self.static = isinstance(lap, int)


class Flow:

    def __init__(self, nc, ctx):
        self.nc, self.ctx, self.sems, self.base = nc, ctx, {}, {}

    def sem(self, name):
        if name not in self.sems:
            self.sems[name] = self.ctx.enter_context(self.nc.semaphore("s_" + name))
            self.base[name] = 0
        return self.sems[name]


class Phase:

    def __init__(self, flow, n_groups):
        self.flow, self.n, self.queue, self.made = flow, n_groups, {}, {}
        self.lag, self.place = 0, 0

    def at(self, lag, place=0):
        self.lag, self.place = lag, place

    def step(self, engine, name, waits, fn):
        self.flow.sem(name)
        self.put(engine, name, waits, fn, 0)

    def dma(self, engine, name, waits, fn, count=1):
        for r in range(RING):
            self.flow.sem(name + str(r))
        self.put(engine, name, waits, fn, count)

    def put(self, engine, name, waits, fn, count):
        assert name not in self.made
        self.made[name] = count
        self.queue.setdefault(engine, []).append((self.place, self.lag, name, waits, fn, count))
        self.place += 1

    def landed(self, name, lap, slot, count):
        s = name + str(slot)
        return self.flow.sem(s), self.flow.base[s] + (lap + 1) * (16 * count)

    def wait(self, eng, q, producer, back):
        k = self.made[producer]
        if q.static and not 0 <= q.g - back < self.n:
            if q.g - back < 0:
                return
            back = q.g - (self.n - 1)
        if k:
            lap, slot = (q.slot - back) // RING, (q.slot - back) % RING
            sem, count = self.landed(producer, q.lap + lap if lap else q.lap, slot, k)
        else:
            sem, count = self.flow.sem(producer), q.g + (1 - back + self.flow.base[producer])
        eng.wait_ge(sem, count)

    def one(self, eng, q, item):
        _, _, name, waits, fn, count = item
        for producer, back in waits:
            self.wait(eng, q, producer, back)
        if waits and name == "gather":
            eng.sem_inc(self.flow.sem("passed"), 1)
        if count and name.startswith("st_") and q.static and q.g == self.n - 1:
            self.wait(eng, q, name, 1)
        if count:
            for d in fn(q):
                d.then_inc(self.flow.sem(name + str(q.slot)), 16)
        else:
            fn(q).then_inc(self.flow.sem(name), 1)

    def sweep(self, eng, items):
        items = sorted(items, key=lambda i: (i[0], -i[1]))
        last = max(i[1] for i in items)
        hi = (self.n - 1) // RING * RING
        lo = min(-(-(last + RING) // RING) * RING, hi)

        def static(j):
            for i in items:
                if 0 <= j - i[1] < self.n:
                    self.one(eng, Group((j - i[1]) // RING, (j - i[1]) % RING), i)

        for j in range(lo):
            static(j)
        if hi > lo:
            with eng.Fori(lo // RING, hi // RING) as lap:
                for r in range(RING):
                    for i in items:
                        back, slot = (r - i[1]) // RING, (r - i[1]) % RING
                        self.one(eng, Group(lap + back if back else lap, slot), i)
        for j in range(hi, self.n + last):
            static(j)

    def run(self, nc):
        with nc.Block() as block:
            marks = {"sp": block.sync, "pool": block.gpsimd, "pe": block.tensor, "dve": block.vector, "act": block.scalar}
            for name, mark in marks.items():
                items = self.queue.get(name, [])
                if not items:
                    continue

                def body(eng, items=items):
                    self.sweep(eng, items)
                    for _, _, label, _, _, count in items:
                        if count:
                            for r in range(RING):
                                lap = (self.n - 1 - r) // RING
                                eng.wait_ge(*self.landed(label, lap, r, count))
                mark(body)
        for name, count in self.made.items():
            if count:
                for r in range(RING):
                    self.flow.base[name + str(r)] += ((self.n - 1 - r) // RING + 1) * 16 * count
            else:
                self.flow.base[name] += self.n


def build_program(nc, a, out):
    n, feat = a["x"].shape
    e = a["src"].shape[0]
    links = e - n
    ng = -(-n // ROWS)
    nt = ng * TILES
    last_base = n - ROWS
    kf = feat // P
    V, S, G, T, D = nc.vector, nc.scalar, nc.gpsimd, nc.tensor, nc.sync

    def dram(name, shape, dt=F32):
        return nc.dram_tensor(name, shape, dt, kind="Internal").ap()

    ctx = ExitStack()
    with ctx:
        def sb(name, shape, dt=F32):
            return ctx.enter_context(nc.sbuf_tensor(name, shape, dt))

        flow = Flow(nc, ctx)
        psum = ctx.enter_context(nc.psum_tensor("psum", [P, 4096], F32))

        def bank(first, count):
            return psum[:, first * 512:(first + count) * 512]

        link_recs = dram("link_recs", [links, 4])
        slot_dst = dram("slot_dst", [nt, P])
        slot_open = dram("slot_open", [nt, P])
        hop_a = dram("hop_a", [n, feat])
        hop_b = dram("hop_b", [n, feat])
        x1 = dram("x1", [n, feat])
        x2 = dram("x2", [n, feat])
        x3 = dram("x3", [n, feat])
        tab1 = dram("tab1", [n, feat])
        recv1 = dram("recv1", [n, feat])
        heads1, cols1 = a["L1_gnn_W_s"].shape[1:]
        heads2, cols2 = a["L2_gnn_att_src"].shape
        heads3, cols3 = a["L3_gnn_att_src"].shape
        f2, f3 = heads2 * cols2, heads3 * cols3
        w2, w3 = f2 + 2 * heads2, f3 + 2 * heads3
        tab2 = dram("tab2", [n, w2])
        tab3 = dram("tab3", [n, w3])

        ident = sb("ident", [P, P])
        iota_row = sb("iota_row", [P, P])
        iota_col = sb("iota_col", [P, 1])
        ones = sb("ones", [P, P])
        base_row = sb("base_row", [P, nt])
        link_src = sb("link_src", [P, nt], I32)
        link_dst = sb("link_dst", [P, nt])
        link_end = sb("link_end", [P, nt])
        inv_deg = sb("inv_deg", [P, nt])
        no_link = sb("no_link", [P, nt])
        power = sb("power", [P, 2 * TILES])
        neg_slope = sb("neg_slope", [P, 1])

        weights = {}

        def weight(name, shape, src):
            weights[name] = (sb(name, shape), src)
            return weights[name][0]

        def chunks(w):
            return w.rearrange("(c p) m -> p c m", p=P)

        def spread(row, m):
            return row.rearrange("(o m) -> o m", o=1).to_broadcast([P, m])

        w_l0a = weight("w_l0a", [P, kf, feat], chunks(a["L0_gnn_W1"]))
        w_l0b = weight("w_l0b", [P, kf, feat], chunks(a["L0_gnn_W2"]))
        w_snd = weight("w_snd", [P, kf, feat], chunks(a["L1_gnn_W_s"].rearrange("d h k -> d (h k)")))
        w_rcv = weight("w_rcv", [P, kf, feat], chunks(a["L1_gnn_W_r"].rearrange("d h k -> d (h k)")))
        w_g2 = weight("w_g2", [P, kf, f2], chunks(a["L2_gnn_W"]))
        w_p2 = weight("w_p2", [P, feat], a["L2_gnn_Wp"])
        w_g3 = weight("w_g3", [P, kf, f3], chunks(a["L3_gnn_W"]))
        b_l0a = weight("b_l0a", [P, feat], spread(a["L0_gnn_b1"], feat))
        b_l0b = weight("b_l0b", [P, feat], spread(a["L0_gnn_b2"], feat))
        b_snd = weight("b_snd", [P, feat], spread(a["L1_gnn_b_s"].rearrange("h k -> (h k)"), feat))
        b_rcv = weight("b_rcv", [P, feat], spread(a["L1_gnn_b_r"].rearrange("h k -> (h k)"), feat))
        a_w = weight("a_w", [P, cols1], spread(a["L1_gnn_a_w"], cols1))
        a_b = weight("a_b", [P, 1], spread(a["L1_gnn_a_b"], 1))
        b_g2 = weight("b_g2", [P, f2], spread(a["L2_gnn_bias"], f2))
        b_p2 = weight("b_p2", [P, feat], spread(a["L2_gnn_bp"], feat))
        b_g3 = weight("b_g3", [P, f3], spread(a["L3_gnn_bias"], f3))
        slope = weight("slope", [P, 1], spread(a["L0_gnn_a"], 1))
        att2 = weight("att2", [P, 2, f2], None)
        att3 = weight("att3", [P, 2, f3], None)
        w_a2 = sb("w_a2", [P, kf, 2, heads2])
        w_a3 = sb("w_a3", [P, kf, 2, heads3])
        att_tmp = sb("att_tmp", [P, max(f2, f3)])

        s_w, s_c = flow.sem("weights"), flow.sem("const")

        step_cols = 2 * STAGE
        raw = -(-e // P)
        ec = -(-raw // step_cols) * step_cols
        tail = e - (P - 1) * raw
        assert 2 < tail <= raw and n >= 2 * ROWS
        with ExitStack() as tmp:
            def tb(name, shape, dt=F32):
                return tmp.enter_context(nc.sbuf_tensor(name, shape, dt))
            src_i = tb("src_i", [P, raw], I32)
            near = [tb(f"dst_i{k}", [P, raw], I32) for k in range(4)]
            nearf = [tb(f"dst_f{k}", [P, raw]) for k in range(4)]
            edge_i = tb("edge_i", [P, raw], I32)
            edge_f = tb("edge_f", [P, raw])
            is_end = tb("is_end", [P, raw])
            recs = tb("recs", [P, ec, 4])
            pos = tb("pos", [P, ec], I32)
            base_i = tb("base_i", [P, nt], I32)
            below = tb("below", [P, 512])
            scratch = tb("scratch", [P, raw])
            first_link = tb("first_link", [P, nt])
            slot_idx = tb("slot_idx", [P, nt], I32)
            recs_t = tb("recs_t", [P, nt, 4])
            row_t = tb("row_t", [P, P])
            open_t = tb("open_t", [P, nt])
            in_tile = tb("in_tile", [P, nt])
            tmp_t = tb("tmp_t", [P, nt])
            pos_stage = tb("pos_stage", [P, 2, STAGE], I32)
            rec_stage = tb("rec_stage", [P, 2, STAGE, 4])
            iota_i = tb("iota_i", [P, P + 1], I32)

            pad_value = [-1, -1, -1, -1]
            s_e, s_pad, s_v = flow.sem("edges"), flow.sem("pad"), flow.sem("setup")
            with nc.Block() as block:
                chain = [0]

                def link(ins):
                    chain[0] += 1
                    ins.then_inc(s_v, 1)
                    V.wait_ge(s_v, chain[0])

                @block.sync
                def _(eng):
                    for handle, src in weights.values():
                        if src is not None:
                            eng.dma_start(handle[:], src).then_inc(s_w, 16)
                    for t, name in ((att2, "L2"), (att3, "L3")):
                        for j, side in enumerate(("src", "dst")):
                            v = a[f"{name}_gnn_att_{side}"].rearrange("h c -> (h c)")
                            eng.dma_start(t[:, j, :], spread(v, v.shape[0])).then_inc(s_w, 16)
                    eng.wait_ge(s_pad, 1)
                    for t, shift, src in [(src_i, 0, a["src"])] + [(near[k], k - 1, a["dst"]) for k in range(4)]:
                        head = max(0, -shift)
                        if head:
                            eng.dma_start(t[0:1, head:raw], src[0:raw - head].rearrange("(o m) -> o m", o=1)).then_inc(s_e, 16)
                            eng.dma_start(t[1:P - 1, :], src[raw - head:(P - 1) * raw - head].rearrange("(p m) -> p m", m=raw)).then_inc(s_e, 16)
                        else:
                            eng.dma_start(t[0:P - 1, :], src[shift:(P - 1) * raw + shift].rearrange("(p m) -> p m", m=raw)).then_inc(s_e, 16)
                        got = min(tail - shift, raw) if shift >= 0 else tail
                        eng.dma_start(t[P - 1:P, 0:got], src[(P - 1) * raw + shift:(P - 1) * raw + shift + got].rearrange("(o m) -> o m", o=1)).then_inc(s_e, 16)
                    eng.wait_ge(s_e, 11 * 16)
                    eng.wait_ge(s_w, 16 * (len(weights) - 2 + 4))

                @block.gpsimd
                def _(eng):
                    for k in range(4):
                        eng.memset(near[k][:], pad_value[k])
                    eng.memset(src_i[:], 0).then_inc(s_pad, 1)
                    eng.memset(ident[:], 0.0)
                    eng.memset(ones[:], 1.0)
                    eng.memset(recs[:], 0.0)
                    eng.memset(pos[:], int(FAR))
                    eng.memset(power[:, 0:TILES], -0.5)
                    eng.memset(power[:, TILES:2 * TILES], 0.5)
                    eng.memset(below[:], 0.0)
                    eng.memset(recs_t[:], -FAR).then_inc(s_pad, 1)
                    eng.iota(edge_i[:], [[1, raw]], base=0, channel_multiplier=raw)
                    full = nt - TILES
                    eng.iota(base_i[:, 0:full], [[P, full]], base=0, channel_multiplier=0)
                    eng.iota(base_i[:, full:nt], [[P, TILES]], base=last_base, channel_multiplier=0)
                    eng.iota(iota_i[:, 0:P], [[1, P]], base=0, channel_multiplier=0)
                    eng.iota(iota_i[:, P:P + 1], [[0, 1]], base=0, channel_multiplier=1).then_inc(s_c, 1)
                    eng.wait_ge(s_pad, 2)
                    eng.affine_select(out=ident[:], in_=ident[:], compare_op=ALU.not_equal, fill=1.0, base=0,
                                      pattern=[[-1, P]], channel_multiplier=1).then_inc(s_c, 1)

                @block.vector
                def _(eng):
                    eng.wait_ge(s_c, 2)
                    V.tensor_copy(iota_row[:], iota_i[:, 0:P])
                    V.tensor_copy(iota_col[:], iota_i[:, P:P + 1])
                    V.tensor_copy(base_row[:], base_i[:])
                    V.tensor_copy(edge_f[:], edge_i[:])
                    eng.wait_ge(s_e, 11 * 16)
                    for k in range(4):
                        V.tensor_copy(nearf[k][:], near[k][:])
                    link(V.tensor_copy(recs[:, 0:raw, 0], src_i[:]))
                    before, here, after, after2 = (t[:] for t in nearf)
                    V.tensor_copy(recs[:, 0:raw, 1], here)
                    V.tensor_tensor(is_end[:], here, after, ALU.not_equal)
                    V.tensor_tensor(edge_f[:], edge_f[:], here, ALU.subtract)
                    V.tensor_tensor(scratch[:], after, after2, ALU.is_equal)
                    link(V.tensor_tensor(recs[:, 0:raw, 3], before, here, ALU.not_equal))
                    link(V.tensor_scalar(scratch[:], scratch[:], -FAR, None, ALU.mult))
                    link(V.tensor_tensor(recs[:, 0:raw, 2], scratch[:], here, ALU.add))
                    link(V.scalar_tensor_tensor(scratch[:], is_end[:], FAR, edge_f[:], ALU.mult, ALU.add))
                    link(V.tensor_copy(pos[:, 0:raw], scratch[:]))
                    eng.wait_ge(s_w, 16 * (len(weights) - 2 + 4))
                    link(V.tensor_scalar(neg_slope[:], slope[:], -1.0, None, ALU.mult))
                    for w, att, wa, heads, width in ((w_g2, att2, w_a2, heads2, f2), (w_g3, att3, w_a3, heads3, f3)):
                        for c in range(kf):
                            for j in range(2):
                                link(V.tensor_tensor(att_tmp[:, 0:width], w[:, c, :], att[:, j, :], ALU.mult))
                                link(V.tensor_reduce(wa[:, c, j, :], att_tmp[:, 0:width].rearrange("p (h c) -> p h c", h=heads),
                                                     AX.X, ALU.add))

            rounds = ec // step_cols
            counts = -(-nt // rounds)
            assert counts * rounds <= 512 and nt <= 512
            s_cnt = flow.sem("count")
            s_stage, s_sent = flow.sem("stage"), [flow.sem("sent0"), flow.sem("sent1")]
            thr = tb("thr", [P, counts * rounds])
            with nc.Block() as block:
                @block.vector
                def _(eng):
                    V.memset(thr[:], 0.0).then_inc(s_pad, 1)
                    eng.wait_ge(s_pad, 3)
                    V.tensor_copy(thr[:, 0:nt], base_row[:]).then_inc(s_pad, 1)
                    eng.wait_ge(s_pad, 4)
                    def one_round(r, first):
                        for half in range(2):
                            if not first:
                                eng.wait_ge(s_sent[half], r * (16 * STAGE))
                            c0 = bass.ds(r * step_cols + half * STAGE, STAGE)
                            V.tensor_copy(pos_stage[:, half, :], pos[:, c0])
                            V.tensor_copy(rec_stage[:, half, :, :], recs[:, c0, :]).then_inc(s_stage, 1)
                        for k in range(counts):
                            t = bass.ds(r * counts + k, 1)
                            V.tensor_scalar(scratch[:], nearf[1][:], thr[:, t], 0.0, ALU.is_lt, ALU.add,
                                            accum_out=below[:, t]).then_inc(s_cnt, 1)
                            eng.wait_ge(s_cnt, r * counts + k + 1)

                    one_round(0, True)
                    with eng.Fori(1, rounds) as r:
                        one_round(r, False)

                @block.gpsimd
                def _(eng):
                    with eng.Fori(0, rounds) as r:
                        for half in range(2):
                            eng.wait_ge(s_stage, r * 2 + half + 1)
                            eng.sem_inc(flow.sem("passed"), 1)
                            for k in range(STAGE):
                                eng.indirect_dma_start(
                                    out=link_recs, out_offset=bass.IndirectOffsetOnAxis(ap=pos_stage[:, half, k:k + 1], axis=0),
                                    in_=rec_stage[:, half, k, :], in_offset=None,
                                    bounds_check=links - 1, oob_is_err=False).then_inc(s_sent[half], 16)
                    for half in range(2):
                        eng.wait_ge(s_sent[half], rounds * 16 * STAGE)

            s_q, s_got = flow.sem("first"), [flow.sem("got0"), flow.sem("got1")]
            s_back = flow.sem("back")
            pads = P * raw - e
            full_rounds = nt // step_cols
            extra = -(-(nt - full_rounds * step_cols) // STAGE)
            got = tb("got", [P, 2, STAGE, 4])
            with nc.Block() as block:
                @block.tensor
                def _(eng):
                    T.matmul(bank(0, 1)[:, 0:nt], ones[:], below[:, 0:nt], start=True, stop=True).then_inc(s_q, 1)

                @block.vector
                def _(eng):
                    link(V.memset(got[:], -FAR))
                    eng.wait_ge(s_q, 1)
                    link(V.tensor_tensor(first_link[:], bank(0, 1)[:, 0:nt], base_row[:], ALU.subtract))
                    link(V.tensor_scalar(first_link[:], first_link[:], iota_col[:, 0:1], float(-pads), ALU.add, ALU.add))
                    V.tensor_copy(slot_idx[:], first_link[:]).then_inc(s_q, 1)
                    eng.wait_ge(s_q, 2)

                    def stage(b, half):
                        V.tensor_copy(pos_stage[:, half, :], slot_idx[:, bass.ds(b, STAGE)]).then_inc(s_stage, 1)

                    def take(b, half, r):
                        eng.wait_ge(s_got[half], (r + 1) * (16 * STAGE))
                        V.tensor_copy(recs_t[:, bass.ds(b, STAGE), :], got[:, half, :, :]).then_inc(s_back, 1)

                    with eng.Fori(0, full_rounds) as r:
                        for half in range(2):
                            stage(r * step_cols + half * STAGE, half)
                        for half in range(2):
                            take(r * step_cols + half * STAGE, half, r)
                    for half in range(extra):
                        b = min(full_rounds * step_cols + half * STAGE, nt - STAGE)
                        stage(b, half)
                        take(b, half, full_rounds)
                    eng.wait_ge(s_back, 2 * full_rounds + extra)
                    V.tensor_tensor(link_end[:], recs_t[:, :, 2], base_row[:], ALU.subtract)
                    V.tensor_scalar(open_t[:], recs_t[:, :, 3], -BIG, None, ALU.mult)
                    link(V.tensor_tensor(link_dst[:], recs_t[:, :, 1], base_row[:], ALU.subtract))
                    V.tensor_scalar(in_tile[:], link_dst[:], -0.5, None, ALU.is_gt)
                    link(V.tensor_scalar(tmp_t[:], link_dst[:], P - 0.5, None, ALU.is_lt))
                    link(V.tensor_tensor(in_tile[:], in_tile[:], tmp_t[:], ALU.mult))
                    link(V.tensor_scalar(tmp_t[:], in_tile[:], -FAR, FAR, ALU.mult, ALU.add))
                    link(V.tensor_tensor(tmp_t[:], tmp_t[:], recs_t[:, :, 0], ALU.add))
                    V.tensor_scalar(tmp_t[:], tmp_t[:], 0.0, None, ALU.max).then_inc(s_q, 1)
                    eng.wait_ge(s_q, 3)
                    V.tensor_copy(link_src[:], tmp_t[:]).then_inc(s_q, 1)

                @block.gpsimd
                def _(eng):
                    def fetch(half, seq):
                        eng.wait_ge(s_stage, 2 * rounds + seq + 1)
                        eng.sem_inc(flow.sem("passed"), 1)
                        for k in range(STAGE):
                            eng.indirect_dma_start(
                                out=got[:, half, k, :], out_offset=None, in_=link_recs,
                                in_offset=bass.IndirectOffsetOnAxis(ap=pos_stage[:, half, k:k + 1], axis=0),
                                bounds_check=links - 1, oob_is_err=False).then_inc(s_got[half], 16)
                    eng.wait_ge(s_q, 2)
                    with eng.Fori(0, full_rounds) as r:
                        for half in range(2):
                            fetch(half, r * 2 + half)
                    for x in range(extra):
                        fetch(x, full_rounds * 2 + x)
                    for half in range(2):
                        eng.wait_ge(s_got[half], (full_rounds + (1 if half < extra else 0)) * 16 * STAGE)

            nb = -(-nt // P)
            bt = nt // nb if nt % nb == 0 else None
            assert bt is not None
            s_tr, s_tc, s_ts = flow.sem("row_tr"), flow.sem("row_cp"), flow.sem("row_st")
            with nc.Block() as block:
                @block.tensor
                def _(eng):
                    for i in range(2 * nb):
                        t = (link_dst, open_t)[i // nb]
                        b = i % nb
                        eng.wait_ge(s_tc, i)
                        T.transpose(bank(0, 1)[0:bt, 0:P], t[:, b * bt:(b + 1) * bt], ident[:]).then_inc(s_tr, 1)

                @block.vector
                def _(eng):
                    for i in range(2 * nb):
                        eng.wait_ge(s_tr, i + 1)
                        eng.wait_ge(s_ts, 16 * i)
                        V.tensor_copy(row_t[0:bt, :], bank(0, 1)[0:bt, 0:P]).then_inc(s_tc, 1)

                @block.sync
                def _(eng):
                    for i in range(2 * nb):
                        d = (slot_dst, slot_open)[i // nb]
                        b = i % nb
                        eng.wait_ge(s_tc, i + 1)
                        eng.dma_start(d[b * bt:(b + 1) * bt, :], row_t[0:bt, :]).then_inc(s_ts, 16)
                    eng.wait_ge(s_ts, 16 * 2 * nb)

        wide = max(feat, w2, w3)
        own_x = sb("own_x", [P, RING, TILES, feat])
        own_t = sb("own_t", [P, RING, TILES * wide])
        got_rows = sb("got_rows", [P, RING, TILES * wide])
        idx = sb("idx", [P, RING, TILES], I32)
        sel = sb("sel", [P, RING, TILES, P])
        sel_end = sb("sel_end", [P, RING, TILES, P])
        sel_t = sb("sel_t", [P, RING, TILES, P])
        own_r = sb("own_r", [P, 2, TILES, feat])
        dst_rows = sb("dst_rows", [P, 2, TILES * P])
        opens = sb("opens", [TILES * heads1, 2, P])
        xt = sb("xt", [P, TILES, kf, P])
        xt_b = sb("xt_b", [P, TILES, kf, P])
        t0 = sb("t0", [P, TILES, feat])
        t1 = sb("t1", [P, TILES, feat])
        t2 = sb("t2", [P, TILES, feat])
        t3 = sb("t3", [P, TILES, feat])
        z = sb("z", [P, 2 * TILES, feat])
        zv = sb("zv", [P, 2 * TILES, feat])
        res = sb("res", [P, 2, TILES, feat])
        tab_o = sb("tab_o", [P, 2, TILES * wide])
        stats = sb("stats", [P, TILES, 6])
        moments = sb("moments", [P, TILES, 5])
        var_eps = sb("var_eps", [P, TILES])
        rstd = sb("rstd", [P, TILES])
        shift = sb("shift", [P, TILES])
        deg = sb("deg", [P, TILES])
        sq = sb("sq", [P, TILES])
        norm_v = sb("norm_v", [P, 3, TILES])
        scanned = sb("scanned", [P, 2, P])

        s_init = flow.sem("init")
        with nc.Block() as block:
            @block.gpsimd
            def _(eng):
                eng.memset(got_rows[:], 0.0).then_inc(s_init, 1)
                eng.memset(scanned[:], 0.0).then_inc(s_init, 1)
                eng.wait_ge(s_init, 2)

        def rows(t, q):
            r0 = min(q.g * ROWS, last_base) if q.static else None
            sl = slice(r0, r0 + ROWS) if q.static else bass.ds(q.g * ROWS, ROWS)
            return t[sl, :].rearrange("(k p) f -> p k f", p=P)

        def tiles(q, k=None):
            c0, m = (q.g * TILES, TILES) if k is None else (q.g * TILES + k, 1)
            return slice(c0, c0 + m) if q.static else bass.ds(c0, m)

        def split(t, par, width):
            return t[:, par, 0:TILES * width].rearrange("p (k w) -> p k w", k=TILES)

        HALF = TILES // 2

        def fetch_links(ph, table, width, done):
            ph.at(0)
            ph.step("dve", "idx", [("gather", 4)], lambda q: V.tensor_copy(idx[:, q.slot, :], link_src[:, tiles(q)]))
            ph.dma("pool", "gather", [("idx", 0), (done, 4)], lambda q: [
                G.indirect_dma_start(out=got_rows[:, q.slot, k * width:(k + 1) * width], out_offset=None, in_=table,
                                     in_offset=bass.IndirectOffsetOnAxis(ap=idx[:, q.slot, k:k + 1], axis=0),
                                     bounds_check=n - 1, oob_is_err=False) for k in range(TILES)], count=TILES)
            ph.step("dve", "sel", [(done, 4)], lambda q: V.tensor_tensor(
                sel[:, q.slot], iota_row[:].unsqueeze(1).to_broadcast([P, TILES, P]),
                link_dst[:, tiles(q)].unsqueeze(2).to_broadcast([P, TILES, P]), ALU.is_equal))

        def transpose_rows(ph, name, src, to, ps, after, ps_free, to_free, chunks_=kf):
            flat = to[:].rearrange("p k c f -> p (k c f)")
            parts = 2 if chunks_ > 1 else 1
            m = TILES // parts
            for h in range(parts):
                def tr(q, h=h):
                    for k in range(m):
                        for c in range(chunks_):
                            o = (k * chunks_ + c) * P
                            i = T.transpose(ps[:, o:o + P], src(q)[:, h * m + k, c * P:(c + 1) * P], ident[:])
                    return i

                def cp(q, h=h):
                    w = m * chunks_ * P
                    return S.copy(flat[:, h * w:(h + 1) * w], ps[:, 0:w])
                ph.step("pe", f"{name}_tr{h}", after + (ps_free if h == 0 else [(f"{name}_xt0", 0)]), tr)
                ph.step("act", f"{name}_xt{h}", [(f"{name}_tr{h}", 0)] + (to_free if h == 0 else []), cp)

        def product(frm, w, width, ps, k0, k1, chunks_=kf, extra=None):
            flat = frm[:].rearrange("p k c f -> p (k c f)")

            def mm(q):
                for k in range(k0, k1):
                    out_ = ps[:, (k - k0) * width:(k - k0 + 1) * width]
                    for c in range(chunks_):
                        o = (k * chunks_ + c) * P
                        i = T.matmul(out_, flat[:, o:o + P], w[:, c, :] if chunks_ > 1 else w[:],
                                     start=(c == 0), stop=(c == chunks_ - 1 and extra is None))
                    if extra is not None:
                        i = T.matmul(out_, ident[:], extra(q, k), start=False, stop=True)
                return i
            return mm

        def layer_norm(ph, src, after, dst, dst_free):
            def st(q):
                for k in range(TILES):
                    i = V.bn_stats(stats[:, k, :], src(q)[:, k, :])
                return i

            def halves(q):
                V.tensor_tensor(moments[:, :, 0], stats[:, :, 1], stats[:, :, 4], ALU.add)
                V.tensor_tensor(moments[:, :, 1], stats[:, :, 1], stats[:, :, 4], ALU.subtract)
                return V.tensor_tensor(moments[:, :, 2], stats[:, :, 2], stats[:, :, 5], ALU.add)

            def parts(q):
                V.tensor_scalar(moments[:, :, 3], moments[:, :, 2], 1.0 / feat, EPS, ALU.mult, ALU.add)
                return V.scalar_tensor_tensor(moments[:, :, 4], moments[:, :, 1], 0.25, moments[:, :, 1], ALU.mult, ALU.mult)

            def ln(q):
                for k in range(TILES):
                    i = S.activation(dst(q)[:, k, :], src(q)[:, k, :], ACT.Identity, bias=shift[:, k:k + 1], scale=rstd[:, k:k + 1])
                return i
            ph.step("dve", "stats", after, st)
            ph.step("dve", "halves", [("stats", 0)], halves)
            ph.step("dve", "parts", [("halves", 0)], parts)
            ph.step("dve", "veps", [("parts", 0)], lambda q: V.tensor_tensor(var_eps[:], moments[:, :, 3], moments[:, :, 4], ALU.add))
            ph.step("pool", "rstd", [("veps", 0), ("ln", 1)], lambda q: G.tensor_tensor(rstd[:], var_eps[:], power[:, 0:TILES], ALU.pow))
            ph.step("dve", "shift", [("rstd", 0)], lambda q: V.scalar_tensor_tensor(
                shift[:], moments[:, :, 0], -0.5, rstd[:], ALU.mult, ALU.mult))
            ph.step("act", "ln", [("shift", 0)] + dst_free, ln)

        def grid(ps, width, m=TILES):
            return ps[:, 0:m * width].rearrange("p (k w) -> p k w", k=m)

        def bc(row, width, m=TILES):
            return row[:, 0:width].unsqueeze(1).to_broadcast([P, m, width])

        def hop(table, kind, outs, first=False):
            ph = Phase(flow, ng)
            agg, tp, dn, dn2 = bank(0, 2), bank(2, 1), bank(4, 2), bank(6, 2)
            mean_row = own_r
            ph.dma("sp", "own_t", [("agg", 4)], lambda q: [D.dma_start(split(own_t, q.slot, feat), rows(table, q))])
            if kind == "x1":
                ph.at(1)
                ph.dma("sp", "own_x", [("add_x", 4)], lambda q: [D.dma_start(own_x[:, q.slot], rows(a["x"], q))])
            fetch_links(ph, table, feat, "agg")

            ph.at(1)

            def sum_links(q):
                g, o_rows = split(got_rows, q.slot, feat), split(own_t, q.slot, feat)
                for k in range(TILES):
                    o = agg[:, k * feat:(k + 1) * feat]
                    T.matmul(o, sel[:, q.slot, k, :], g[:, k, :], start=True, stop=False)
                    i = T.matmul(o, ident[:], o_rows[:, k, :], start=False, stop=True)
                    if first:
                        i = T.matmul(dn[:, k:k + 1], sel[:, q.slot, k, :], ones[:, 0:1], start=True, stop=True)
                return i
            ph.step("pe", "agg", [("own_t", 0), ("gather", 0), ("sel", 0), ("mean", 1)] + ([("no_link", 1)] if first else []), sum_links)
            if first:
                ph.step("dve", "deg", [("agg", 0)], lambda q: V.tensor_scalar(deg[:], dn[:, 0:TILES], 1.0, None, ALU.add))
                ph.step("dve", "no_link", [("deg", 0)], lambda q: V.tensor_scalar(
                    no_link[:, tiles(q)], dn[:, 0:TILES], 0.5, -BIG, ALU.is_lt, ALU.mult))
                ph.step("dve", "inv", [("deg", 0)], lambda q: V.reciprocal(inv_deg[:, tiles(q)], deg[:]))

            def mean(q):
                for k in range(TILES):
                    i = S.mul(mean_row[:, q.par, k, :], agg[:, k * feat:(k + 1) * feat], inv_deg[:, tiles(q, k)])
                return i
            mean_free = ("st_a", 2) if kind == "hop" else ("up_tr1", 2)
            ph.step("act", "mean", [("agg", 0), mean_free] + ([("inv", 0)] if first else []), mean)
            if kind == "hop":
                ph.dma("act", "st_a", [("mean", 0)], lambda q: [S.dma_start(rows(outs[0], q), mean_row[:, q.par])])
                ph.run(nc)
                return
            w, b = (w_l0a, b_l0a) if kind == "h1" else (w_l0b, b_l0b)
            ph.at(2)
            transpose_rows(ph, "up", lambda q: mean_row[:, q.par], xt, tp, [("mean", 0)], [("up_xt1", 1)], [("up_mm", 1)])
            ph.step("pe", "up_mm", [("up_xt1", 0), ("pre_b" if kind == "x1" else "biased", 1)], product(xt, w, feat, dn, 0, TILES))
            if kind == "x1":
                ph.step("dve", "pre_b", [("up_mm", 0), ("neg", 1)], lambda q: V.tensor_tensor(t0[:], grid(dn, feat), bc(b, feat), ALU.add))
                ph.step("dve", "biased", [("pre_b", 0), ("own_x", 0)], lambda q: V.tensor_tensor(t0[:], t0[:], own_x[:, q.slot], ALU.add))
            else:
                ph.step("dve", "biased", [("up_mm", 0), ("neg", 1)], lambda q: V.tensor_tensor(t0[:], grid(dn, feat), bc(b, feat), ALU.add))
            ph.step("act", "pos", [("biased", 0), ("prelu", 1)], lambda q: S.activation(t1[:], t0[:], ACT.Relu))
            ph.step("act", "neg", [("biased", 0)], lambda q: S.activation(t2[:], t0[:], ACT.Relu, scale=-1.0))
            if kind == "h1":
                ph.step("dve", "prelu", [("neg", 0), ("st_a", 2)], lambda q: V.scalar_tensor_tensor(
                    res[:, q.par], t2[:], neg_slope[:, 0:1], t1[:], ALU.mult, ALU.add))
                ph.dma("act", "st_a", [("prelu", 0)], lambda q: [S.dma_start(rows(outs[0], q), res[:, q.par])])
                ph.run(nc)
                return
            ph.step("dve", "prelu", [("neg", 0), ("ln", 1)], lambda q: V.scalar_tensor_tensor(
                t3[:], t2[:], neg_slope[:, 0:1], t1[:], ALU.mult, ALU.add))
            ph.at(3)
            ph.step("dve", "add_x", [("prelu", 0)], lambda q: V.tensor_tensor(t3[:], t3[:], own_x[:, q.slot], ALU.add))
            layer_norm(ph, lambda q: t3, [("add_x", 0)], lambda q: res[:, q.par], [("st_a", 2), ("x1_tr1", 2)])
            ph.dma("act", "st_a", [("ln", 0)], lambda q: [S.dma_start(rows(outs[0], q), res[:, q.par])])
            ph.at(4)
            tp2 = bank(3, 1)
            transpose_rows(ph, "x1", lambda q: res[:, q.par], xt_b, tp2, [("ln", 0)], [("x1_xt1", 1)], [("rcv_mm", 1)])
            ph.step("pe", "snd_mm", [("x1_xt1", 0), ("rcv", 1)], product(xt_b, w_snd, feat, dn2, 0, TILES))
            ph.step("dve", "snd", [("snd_mm", 0), ("st_s", 2)], lambda q: V.tensor_tensor(split(tab_o, q.par, feat), grid(dn2, feat), bc(b_snd, feat), ALU.add))
            ph.dma("act", "st_s", [("snd", 0)], lambda q: [S.dma_start(rows(outs[1], q), split(tab_o, q.par, feat))])
            ph.step("pe", "rcv_mm", [("snd", 0)], product(xt_b, w_rcv, feat, dn2, 0, TILES))
            ph.step("dve", "rcv", [("rcv_mm", 0), ("st_r", 2)], lambda q: V.tensor_tensor(
                zv[:, q.par * TILES:(q.par + 1) * TILES, :], grid(dn2, feat), bc(b_rcv, feat), ALU.add))
            ph.dma("act", "st_r", [("rcv", 0)], lambda q: [S.dma_start(rows(outs[2], q), zv[:, q.par * TILES:(q.par + 1) * TILES, :])])
            ph.run(nc)

        small_names = ("maxes", "mx", "d_self", "d_link", "den", "inv", "w_link", "w_self")
        gat_small = {k: sb("g_" + k, [P, TILES, heads1]) for k in small_names}
        p_self = sb("p_self", [P, 2, TILES, heads1])
        p_link = sb("p_link", [P, 2, TILES, heads1])
        logits = sb("logits", [P, 2, 2 * TILES, heads1])
        flat_logits = {h: sb(f"flat_logits{h}", [P, TILES * h]) for h in {heads1, heads2, heads3}}

        def gat(xin, table, width, heads, cols, loops, finish, v2=False):
            ph = Phase(flow, ng)
            TA = 5 if finish == "project" else 4
            x_done = {"x2": "agg", "project": "o_mm1", "out": "x_read"}[finish]
            f = heads * cols
            hk = TILES * heads
            agg_ps, spread_ps, sum_ps, tp, dn, log_ps, max_ps = (
                bank(0, 2), bank(2, 1), bank(3, 1), bank(4, 1), bank(5, 1), bank(6, 1), bank(7, 1))
            if finish == "project":
                agg_ps, o_ps = bank(0, 1), bank(1, 1)

            def field(ps, i):
                return ps[:, P + i * 64:P + i * 64 + hk].rearrange("p (k h) -> p k h", k=TILES)
            tmp = {k: v[:, :, 0:heads] for k, v in gat_small.items()}
            ps_ = lambda q: p_self[:, q.par, :, 0:heads]
            pl_ = lambda q: p_link[:, q.par, :, 0:heads]
            le = lambda q: logits[:, q.par, 0:TILES, 0:heads]
            ls = lambda q: logits[:, q.par, TILES:2 * TILES, 0:heads]
            lflat = flat_logits[heads]

            def slot_rows(t, q):
                c0 = q.g * TILES
                return t[slice(c0, c0 + TILES) if q.static else bass.ds(c0, TILES), :]
            ph.at(0)
            ph.dma("sp", "own_t", [("v_self", 4)], lambda q: [D.dma_start(split(own_t, q.slot, width), rows(table, q))])
            if v2:
                ph.dma("sp", "own_r", [("z_self", 2), ("spread_r1", 2)], lambda q: [D.dma_start(own_r[:, q.par], rows(recv1, q))])
            ph.dma("sp", "dst_row", [("sel_t", 2)], lambda q: [D.dma_start(
                dst_rows[:, q.par, :], slot_rows(slot_dst, q).rearrange("(o k) s -> o (k s)", o=1).to_broadcast([P, TILES * P]))])
            ph.dma("sp", "open_row", [("scan", 2)], lambda q: [D.dma_start(
                opens[k * heads:(k + 1) * heads, q.par, :], slot_rows(slot_open, q)[k:k + 1, :].to_broadcast([heads, P])) for k in range(TILES)], count=TILES)
            ph.at(1)
            ph.dma("sp", "own_x", [(x_done, 4)], lambda q: [D.dma_start(own_x[:, q.slot], rows(xin, q))])
            fetch_links(ph, table, width, "agg")
            ph.step("dve", "sel_t", [("dst_row", 0), ("agg", 4)], lambda q: V.tensor_scalar(
                sel_t[:, q.slot].rearrange("p k s -> p (k s)"), dst_rows[:, q.par, :], iota_col[:, 0:1], None, ALU.is_equal))
            ph.step("dve", "sel_end", [("agg", 4)], lambda q: V.tensor_tensor(
                sel_end[:, q.slot], iota_row[:].unsqueeze(1).to_broadcast([P, TILES, P]),
                link_end[:, tiles(q)].unsqueeze(2).to_broadcast([P, TILES, P]), ALU.is_equal))

            def each(out, lhs, rhs, k0=0, k1=TILES):
                def go(q):
                    for k in range(k0, k1):
                        i = T.matmul(out(q)[:, k - k0, :], lhs[:, q.slot, k, :], rhs(q)[:, k, :], start=True, stop=True)
                    return i
                return go

            ph.at(1)
            if v2:
                z3 = z[:].rearrange("p k (h c) -> p (k h) c", c=cols)
                ph.step("dve", "z_self", [("own_r", 0), ("own_t", 0), ("z_sum", 1)], lambda q: V.tensor_tensor(
                    z[:, TILES:2 * TILES, :], split(own_t, q.slot, feat), own_r[:, q.par], ALU.add))
                for h in range(2):
                    ph.step("pe", f"spread_r{h}", [("own_r", 0), ("sel_t", 0), ("z_link0", 0) if h else ("z_link1", 1)],
                            each(lambda q: grid(spread_ps, feat, HALF), sel_t, lambda q: own_r[:, q.par], h * HALF, (h + 1) * HALF))
                    ph.step("dve", f"z_link{h}", [(f"spread_r{h}", 0), ("gather", 0)], lambda q, h=h: V.tensor_tensor(
                        z[:, h * HALF:(h + 1) * HALF, :], grid(spread_ps, feat, HALF),
                        split(got_rows, q.slot, feat)[:, h * HALF:(h + 1) * HALF, :], ALU.add))
                ph.step("dve", "leaky", [("z_link1", 0)], lambda q: V.scalar_tensor_tensor(z[:], z[:], 0.01, z[:], ALU.mult, ALU.max))
                ph.step("dve", "z_w", [("leaky", 0)], lambda q: V.tensor_tensor(
                    z3, z3, a_w[:].unsqueeze(1).to_broadcast([P, 2 * TILES * heads, cols]), ALU.mult))
                ph.step("dve", "z_sum", [("z_w", 0)], lambda q: V.tensor_reduce(
                    logits[:, q.par].rearrange("p k h -> p (k h)"), z3, AX.X, ALU.add))
                ph.step("dve", "logit", [("z_sum", 0)], lambda q: V.tensor_scalar(
                    logits[:, q.par], logits[:, q.par], a_b[:, 0:1], None, ALU.add))
            else:
                ph.step("pe", "spread_a", [("own_t", 0), ("sel_t", 0), ("scan", 1)] + ([] if finish == "out" else [("t_a", TA)]), each(
                    lambda q: field(log_ps, 0), sel_t, lambda q: split(own_t, q.slot, width)[:, :, f + heads:f + 2 * heads]))
                ph.step("dve", "z_self", [("own_t", 0)], lambda q: V.tensor_tensor(
                    ls(q), split(own_t, q.slot, width)[:, :, f:f + heads], split(own_t, q.slot, width)[:, :, f + heads:f + 2 * heads], ALU.add))
                ph.step("dve", "z_link", [("spread_a", 0), ("gather", 0)], lambda q: V.tensor_tensor(
                    le(q), field(log_ps, 0), split(got_rows, q.slot, width)[:, :, f:f + heads], ALU.add))
                lg = lambda q: logits[:, q.par, :, 0:heads]
                ph.step("dve", "logit", [("z_link", 0), ("z_self", 0)], lambda q: V.scalar_tensor_tensor(
                    lg(q), lg(q), 0.2, lg(q), ALU.mult, ALU.max))
            ph.step("dve", "l_flat", [("logit", 0), ("l_tr", 1)], lambda q: V.tensor_copy(lflat[:].rearrange("p (k h) -> p k h", k=TILES), le(q)))
            ph.step("pe", "l_tr", [("l_flat", 0), ("scan", 1)] + ([("t_a", TA)] if v2 else []), lambda q: T.transpose(log_ps[0:hk, 0:P], lflat[:], ident[:]))
            ph.step("dve", "scan", [("l_tr", 0), ("open_row", 0), ("s_tr", 2)], lambda q: V.tensor_tensor_scan(
                scanned[0:hk, q.par, :], opens[0:hk, q.par, :], log_ps[0:hk, 0:P], -BIG, ALU.add, ALU.max))
            log_done = ph.place

            ph.at(2)
            ph.step("pe", "s_tr", [("scan", 0), ("d_link0", 1)], lambda q: T.matmul(
                field(max_ps, 0).rearrange("p k h -> p (k h)"), scanned[:, q.par, :], ident[:, 0:hk], start=True, stop=True))
            ph.step("act", "s_back", [("s_tr", 0), ("seg_max", 1)], lambda q: S.copy(tmp["maxes"], field(max_ps, 0)))
            ph.step("pe", "seg_max", [("s_back", 0), ("sel_end", 0)], each(lambda q: field(max_ps, 1), sel_end, lambda q: tmp["maxes"]))
            ph.step("dve", "mx0", [("seg_max", 0), ("spread_m", 1)], lambda q: V.tensor_tensor(
                tmp["mx"], field(max_ps, 1), no_link[:, tiles(q)].unsqueeze(2).to_broadcast([P, TILES, heads]), ALU.add))
            ph.step("dve", "mx", [("mx0", 0)], lambda q: V.tensor_tensor(tmp["mx"], tmp["mx"], ls(q), ALU.max))
            ph.step("pe", "spread_m", [("mx", 0)], each(lambda q: field(max_ps, 2), sel_t, lambda q: tmp["mx"]))
            ph.step("dve", "d_self", [("mx", 0), ("p_self", 1)], lambda q: V.tensor_tensor(tmp["d_self"], ls(q), tmp["mx"], ALU.subtract))
            ph.step("act", "p_self", [("d_self", 0), ("w_self", 2)], lambda q: S.activation(ps_(q), tmp["d_self"], ACT.Exp))
            ph.step("dve", "d_link0", [("spread_m", 0), ("p_link", 1)], lambda q: V.tensor_tensor(tmp["d_link"], le(q), field(max_ps, 2), ALU.subtract))
            ph.step("dve", "d_link", [("d_link0", 0)], lambda q: V.tensor_scalar(tmp["d_link"], tmp["d_link"], 0.0, None, ALU.min))
            ph.step("act", "p_link", [("d_link", 0), ("w_link", 2), ("sum_p", 2)], lambda q: S.activation(pl_(q), tmp["d_link"], ACT.Exp))

            ph.at(3)
            ph.step("pe", "sum_p", [("p_link", 0), ("w_link", 1)], each(lambda q: field(sum_ps, 0), sel, pl_))
            ph.step("dve", "den0", [("sum_p", 0), ("p_self", 0)], lambda q: V.scalar_tensor_tensor(
                tmp["den"], ps_(q), float(loops), field(sum_ps, 0), ALU.mult, ALU.add))
            ph.step("dve", "den", [("den0", 0)], lambda q: V.tensor_scalar(tmp["den"], tmp["den"], 1e-16 if finish == "project" else 0.0, None, ALU.add))
            ph.step("dve", "inv_d", [("den", 0), ("spread_i", 1)], lambda q: V.reciprocal(tmp["inv"], tmp["den"]))
            ph.step("pe", "spread_i", [("inv_d", 0)], each(lambda q: field(sum_ps, 1), sel_t, lambda q: tmp["inv"]))
            ph.step("dve", "w_self", [("inv_d", 0)], lambda q: V.scalar_tensor_tensor(
                tmp["w_self"], ps_(q), float(loops), tmp["inv"], ALU.mult, ALU.mult))
            ph.step("dve", "w_link", [("spread_i", 0)], lambda q: V.tensor_tensor(tmp["w_link"], pl_(q), field(sum_ps, 1), ALU.mult))
            zl = zv[:, 0:TILES, 0:f]
            zs = zv[:, TILES:2 * TILES, 0:f]

            def heads4(v):
                return v.rearrange("p k (h c) -> p k h c", c=cols)
            ph.step("dve", "v_self", [("w_self", 0), ("agg", 1)], lambda q: V.tensor_tensor(
                heads4(zs), heads4(split(own_t, q.slot, width)[:, :, 0:f]),
                tmp["w_self"].unsqueeze(3).to_broadcast([P, TILES, heads, cols]), ALU.mult))
            ph.step("dve", "v_link", [("w_link", 0), ("agg", 1)], lambda q: V.tensor_tensor(
                heads4(zl), heads4(split(got_rows, q.slot, width)[:, :, 0:f]),
                tmp["w_link"].unsqueeze(3).to_broadcast([P, TILES, heads, cols]), ALU.mult))

            def agg(q):
                for k in range(TILES):
                    o = agg_ps[:, k * f:(k + 1) * f]
                    T.matmul(o, sel[:, q.slot, k, :], zl[:, k, :], start=True, stop=False)
                    i = T.matmul(o, ident[:], zs[:, k, :], start=False, stop=not v2)
                    if v2:
                        i = T.matmul(o, ident[:], own_x[:, q.slot, k, :], start=False, stop=True)
                return i
            ph.step("pe", "agg", [("v_self", 0), ("v_link", 0)] + ([("own_x", 0), ("ln", 1)] if v2 else [("out_b", 1)]), agg)
            agg_v = grid(agg_ps, f)

            def table_out(nxt_w, nxt_wa, nf, nheads, nwidth, dst, xsrc):
                ph.at(TA)
                o = lambda q: split(tab_o, q.par, nwidth)
                transpose_rows(ph, "t", xsrc, xt, tp, [("ln", 0)], [("t_xt1", 1)], [("t_mm", 1)])
                parts = TILES * nf // 512
                m = TILES // parts
                for h in range(parts):
                    ph.step("pe", f"t_mm{h}", [("t_xt1", 0), (f"t_h{h - 1}", 0) if h else (f"t_h{parts - 1}", 1)],
                            product(xt, nxt_w, nf, dn, h * m, (h + 1) * m))
                    ph.step("act", f"t_h{h}", [(f"t_mm{h}", 0), ("st_t", 2)], lambda q, h=h: S.copy(
                        o(q)[:, h * m:(h + 1) * m, 0:nf], grid(dn, nf, m)))
                att = log_ps[:, 0:TILES * 2 * nheads]

                def mm(q):
                    for k in range(TILES):
                        for c in range(kf):
                            i = T.matmul(att[:, k * 2 * nheads:(k + 1) * 2 * nheads], xt[:, k, c, :],
                                         nxt_wa[:, c].rearrange("p j h -> p (j h)"), start=(c == 0), stop=(c == kf - 1))
                    return i
                ph.place = max(ph.place, log_done)
                ph.step("pe", "t_mm", [("t_xt1", 0), ("scan", 1 - TA)], mm)
                ph.step("act", "t_a", [("t_mm", 0), ("st_t", 2)], lambda q: S.copy(
                    o(q)[:, :, nf:nwidth], att.rearrange("p (k w) -> p k w", k=TILES)))
                ph.dma("act", "st_t", [(f"t_h{parts - 1}", 0), ("t_a", 0)], lambda q: [S.dma_start(rows(dst, q), o(q))])

            if finish == "x2":
                layer_norm(ph, lambda q: agg_v, [("agg", 0)], lambda q: res[:, q.par], [("st_a", 2), ("t_tr1", 2)])
                ph.dma("act", "st_a", [("ln", 0)], lambda q: [S.dma_start(rows(x2, q), res[:, q.par])])
                table_out(w_g2, w_a2, f2, heads2, w2, tab2, lambda q: res[:, q.par])
            elif finish == "project":
                ph.step("dve", "out_b", [("agg", 0), ("o_tr0", 1)], lambda q: V.tensor_tensor(t0[:, :, 0:f], agg_v, bc(b_g2, f), ALU.add))
                ph.at(4)
                transpose_rows(ph, "o", lambda q: t0, xt_b, o_ps, [("out_b", 0)], [("o_xt0", 1)], [("o_mm1", 1)], chunks_=1)
                for h in range(2):
                    ph.step("pe", f"o_mm{h}", [("o_xt0", 0), ("own_x", 0), ("out0", 0) if h else ("out1", 1)],
                            product(xt_b, w_p2, feat, spread_ps, h * HALF, (h + 1) * HALF, chunks_=1, extra=lambda q, k: own_x[:, q.slot, k, :]))
                    ph.step("dve", f"out{h}", [(f"o_mm{h}", 0), ("ln", 1)], lambda q, h=h: V.tensor_tensor(
                        t3[:, h * HALF:(h + 1) * HALF, :], grid(spread_ps, feat, HALF), bc(b_p2, feat, HALF), ALU.add))
                layer_norm(ph, lambda q: t3, [("out1", 0)], lambda q: res[:, q.par], [("st_a", 2), ("t_tr1", 2)])
                ph.dma("act", "st_a", [("ln", 0)], lambda q: [S.dma_start(rows(x3, q), res[:, q.par])])
                table_out(w_g3, w_a3, f3, heads3, w3, tab3, lambda q: res[:, q.par])
            else:
                ph.step("dve", "out_b", [("agg", 0), ("relu", 1)], lambda q: V.tensor_tensor(t0[:], agg_v, bc(b_g3, f), ALU.add))
                ph.step("act", "relu", [("out_b", 0), ("x_read", 2)], lambda q: S.activation((t1, t2)[q.par][:], t0[:], ACT.Relu))

                def square(q):
                    for k in range(TILES):
                        i = S.activation(z[:, k, :], (t1, t2)[q.par][:, k, :], ACT.Square, accum_out=sq[:, k:k + 1])
                    return i
                ph.at(4)
                ph.step("act", "sq", [("relu", 0), ("norm", 1)], square)
                ph.step("pool", "norm", [("sq", 0), ("norm_c", 1)], lambda q: G.tensor_tensor(norm_v[:, 0, :], sq[:], power[:, TILES:2 * TILES], ALU.pow))
                ph.step("dve", "norm_c", [("norm", 0)], lambda q: V.tensor_scalar(norm_v[:, 1, :], norm_v[:, 0, :], 1e-12, None, ALU.max))
                ph.step("dve", "inv_n", [("norm_c", 0)], lambda q: V.reciprocal(norm_v[:, 2, :], norm_v[:, 1, :]))

                def add_x(q):
                    for k in range(TILES):
                        i = V.scalar_tensor_tensor(t3[:, k, :], (t1, t2)[q.par][:, k, :], norm_v[:, 2, k:k + 1], own_x[:, q.slot, k, :], ALU.mult, ALU.add)
                    return i
                ph.step("dve", "x_read", [("inv_n", 0), ("own_x", 0), ("ln", 1)], add_x)
                layer_norm(ph, lambda q: t3, [("x_read", 0)], lambda q: res[:, q.par], [("st_a", 2)])
                ph.dma("act", "st_a", [("ln", 0)], lambda q: [S.dma_start(rows(out, q), res[:, q.par])])
            ph.run(nc)

        hop(a["x"], "hop", [hop_a], first=True)
        hop(hop_a, "h1", [hop_b])
        hop(hop_b, "hop", [hop_a])
        hop(hop_a, "x1", [x1, tab1, recv1])
        gat(x1, tab1, feat, heads1, cols1, 1, "x2", v2=True)
        gat(x2, tab2, w2, heads2, cols2, 2, "project")
        gat(x3, tab3, w3, heads3, cols3, 2, "out")


INPUTS = ["x", "src", "dst", "L0_gnn_W1", "L0_gnn_b1", "L0_gnn_W2", "L0_gnn_b2", "L0_gnn_a", "L1_gnn_W_s", "L1_gnn_b_s",
          "L1_gnn_W_r", "L1_gnn_b_r", "L1_gnn_a_w", "L1_gnn_a_b", "L2_gnn_W", "L2_gnn_att_src", "L2_gnn_att_dst",
          "L2_gnn_bias", "L2_gnn_Wp", "L2_gnn_bp", "L3_gnn_W", "L3_gnn_att_src", "L3_gnn_att_dst", "L3_gnn_bias"]


def kernel(**inputs):
    import concourse.bacc as bacc
    from concourse.bass_utils import run_bass_kernel_spmd

    nc = bacc.Bacc("TRN2", target_bir_lowering=False, num_devices=1)
    arrays, args = {}, {}
    for name in INPUTS:
        v = np.ascontiguousarray(inputs[name])
        arrays["in_" + name] = v
        args[name] = nc.dram_tensor("in_" + name, v.shape, mybir.dt.from_np(v.dtype), kind="ExternalInput").ap()
    out = nc.dram_tensor("out", args["x"].shape, F32, kind="ExternalOutput").ap()
    build_program(nc, args, out)
    return run_bass_kernel_spmd(nc, [arrays], core_ids=[0]).results[0]["out"]
```

```python
from contextlib import ExitStack

import numpy as np
import concourse.bass as bass
from concourse import mybir

P = 128
TILES = 4
ROWS = TILES * P
F32 = mybir.dt.float32
I32 = mybir.dt.int32
ALU = mybir.AluOpType
ACT = mybir.ActivationFunctionType
AX = mybir.AxisListType
FAR = float(2 ** 20)
BIG = 1.0e30
EPS = 1e-5
STAGE = 8


ORDER = {
    "first": (
        "idx:0 agg:3 gather:0 sel:2 own_t:0 deg:3 no_link:3 inv:3 sums:3 mean:3 st_a:3"),
    "h1": (
        "idx:0 prelu:3 up_tr0:3 gather:0 up_xt0:3 up_mm:4 own_t:0 sums:2 biased:2 pos:2 up_tr1:3 neg:2 up_xt1:3 mean:4 "
        "st_a:4 agg:1 sel:0"),
    "hop": (
        "sel:0 idx:0 sums:3 gather:0 agg:1 own_t:0 mean:3 st_a:3"),
    "x1": (
        "sel:0 sums:2 add_x:4 own_t:1 pos:3 x1_xt1:5 own_x:1 stats:4 halves:4 parts:4 idx:0 veps:4 rstd:4 neg:3 pre_b:2 "
        "rcv_mm:5 st_a:5 gather:0 snd_mm:5 shift:4 rcv:5 ln:4 x1_tr0:4 x1_xt0:4 biased:2 prelu:3 st_r:5 agg:1 snd:5 "
        "st_s:5 x1_tr1:4"),
    "x2": (
        "idx:0 sum_p:5 den0:5 agg:6 d_link:4 scan:3 den:5 own_x:5 t_xt0:8 leaky_link:2 z_w:2 gather:0 z_sum:2 dst_row:0 "
        "t_tr1:8 s_tr:3 s_back:3 inv_d:5 z_link0:1 t_xt1:8 p_link:4 own_t:0 w_self:5 z_self:1 down_own:1 spread_i:5 "
        "stats:6 logit:2 w_link:5 halves:6 spread_r1:1 own_r:0 t_mm:8 up_own:1 parts:6 veps:6 v_self:5 z_link1:1 "
        "open_row:1 sel:0 t_tr0:7 t_a:8 seg_max:3 st_a:7 t_mm0:8 sel_t:0 up_link:1 spread_r0:0 l_flat:2 rstd:6 shift:6 "
        "leaky_own:1 down_link:1 d_self:4 mx0:3 ln:6 v_link:5 p_self:4 mx:3 sel_end:2 spread_m:3 t_h0:8 l_tr:2 "
        "d_link0:3 st_t:8"),
    "project": (
        "idx:0 stats:7 t_tr0:8 spread_a:1 seg_max:3 halves:7 d_link:4 parts:7 out0:6 mx0:3 mx:3 l_flat:2 z_link:1 agg:5 "
        "out_b:5 t_xt0:8 t_tr1:8 veps:7 p_self:4 o_mm1:6 p_link:4 sum_p:4 t_xt1:8 l_tr:2 den0:4 o_tr0:5 scan:2 own_t:0 "
        "s_tr:2 logit:1 t_mm0:8 den:4 inv_d:4 dst_row:0 out1:6 s_back:2 gather:0 sel_end:1 own_x:4 spread_i:4 o_xt0:5 "
        "spread_m:3 t_mm:8 t_h0:8 rstd:7 out_x:6 sel:1 open_row:1 shift:7 ln:7 sel_t:0 w_link:4 w_self:4 d_self:3 "
        "v_self:4 t_a:8 v_link:4 z_self:0 o_mm0:5 d_link0:3 st_a:7 t_mm1:8 t_h1:8 st_t:8"),
    "out": (
        "relu:7 mx0:4 sum_p:5 v_self:6 dst_row:0 den0:5 idx:0 v_link:6 mx:4 z_link:2 sel_t:1 spread_m:4 den:5 x_read:8 "
        "logit:2 d_self:4 l_tr:3 d_link0:4 p_self:4 agg:6 gather:0 stats:8 own_x:6 sel_end:3 sq:7 halves:8 scan:3 "
        "d_link:4 inv_d:5 spread_i:5 p_link:4 norm:7 parts:8 sel:2 veps:8 rstd:8 l_flat:2 w_self:5 s_tr:3 z_self:1 "
        "open_row:1 norm_c:7 w_link:5 s_back:3 seg_max:3 out_b:6 shift:8 ln:8 inv_n:7 own_t:0 st_a:8 spread_a:1"),
}
RING = 6


class Group:

    def __init__(self, lap, slot):
        self.lap, self.slot, self.tri, self.par = lap, slot, slot % 3, slot % 2
        self.g = RING * lap + slot
        self.static = isinstance(lap, int)


class Flow:

    def __init__(self, nc, ctx):
        self.nc, self.ctx, self.sems, self.base = nc, ctx, {}, {}

    def sem(self, name):
        if name not in self.sems:
            self.sems[name] = self.ctx.enter_context(self.nc.semaphore("s_" + name))
            self.base[name] = 0
        return self.sems[name]


class Phase:

    def __init__(self, flow, n_groups, order=None):
        self.flow, self.n, self.queue, self.made = flow, n_groups, {}, {}
        self.lag, self.place = 0, 0
        self.order = {}
        for place, item in enumerate((order or "").split()):
            name, lag = item.split(":")
            self.order[name] = (place, int(lag))

    def at(self, lag, place=0):
        self.lag, self.place = lag, place

    def step(self, engine, name, waits, fn):
        self.flow.sem(name)
        self.put(engine, name, waits, fn, 0)

    def dma(self, engine, name, waits, fn, count=1, depth=2):
        for r in range(depth):
            self.flow.sem(name + str(r))
        self.put(engine, name, waits, fn, (count, depth))

    def put(self, engine, name, waits, fn, made):
        assert name not in self.made
        self.made[name] = made
        place, lag = self.order[name] if self.order else (self.place, self.lag)
        self.queue.setdefault(engine, []).append((place, lag, name, waits, fn, made))
        self.place += 1

    def landed(self, name, lap, slot):
        count, depth = self.made[name]
        s = name + str(slot % depth)
        return self.flow.sem(s), lap * (RING // depth * 16 * count) + ((slot // depth + 1) * 16 * count + self.flow.base[s])

    def wait(self, eng, q, producer, back):
        k = self.made[producer]
        if q.static and not 0 <= q.g - back < self.n:
            if q.g - back < 0:
                return
            back = q.g - (self.n - 1)
        if k:
            lap, slot = (q.slot - back) // RING, (q.slot - back) % RING
            sem, count = self.landed(producer, q.lap + lap if lap else q.lap, slot)
        else:
            sem, count = self.flow.sem(producer), q.g + (1 - back + self.flow.base[producer])
        eng.wait_ge(sem, count)

    def one(self, eng, q, item):
        _, _, name, waits, fn, made = item
        for producer, back in waits:
            self.wait(eng, q, producer, back)
        if waits and name == "gather":
            eng.sem_inc(self.flow.sem("passed"), 1)
        if made and name.startswith("st_") and q.static and q.g == self.n - 1:
            self.wait(eng, q, name, 1)
        if made:
            for d in fn(q):
                d.then_inc(self.flow.sem(name + str(q.slot % made[1])), 16)
        else:
            fn(q).then_inc(self.flow.sem(name), 1)

    def sweep(self, eng, items):
        items = sorted(items, key=lambda i: (i[0], -i[1]))
        last = max(i[1] for i in items)
        hi = (self.n - 1) // RING * RING
        lo = min(-(-(last + RING) // RING) * RING, hi)

        def static(j):
            for i in items:
                if 0 <= j - i[1] < self.n:
                    self.one(eng, Group((j - i[1]) // RING, (j - i[1]) % RING), i)

        for j in range(lo):
            static(j)
        if hi > lo:
            with eng.Fori(lo // RING, hi // RING) as lap:
                for r in range(RING):
                    for i in items:
                        back, slot = (r - i[1]) // RING, (r - i[1]) % RING
                        self.one(eng, Group(lap + back if back else lap, slot), i)
        for j in range(hi, self.n + last):
            static(j)

    def run(self, nc, besides=None):
        with nc.Block() as block:
            marks = {"sp": block.sync, "pool": block.gpsimd, "pe": block.tensor, "dve": block.vector, "act": block.scalar}
            for name, mark in marks.items():
                if besides and name in besides:
                    mark(besides[name])
                items = self.queue.get(name, [])
                if not items:
                    continue

                def body(eng, items=items):
                    self.sweep(eng, items)
                    for _, _, label, _, _, made in items:
                        if made:
                            for g in range(self.n - made[1], self.n):
                                eng.wait_ge(*self.landed(label, g // RING, g % RING))
                mark(body)
        for name, made in self.made.items():
            if made:
                count, depth = made
                for r in range(depth):
                    self.flow.base[name + str(r)] += ((self.n - 1 - r) // depth + 1) * 16 * count
            else:
                self.flow.base[name] += self.n


def build_program(nc, a, out):
    n, feat = a["x"].shape
    e = a["src"].shape[0]
    links = e - n
    ng = -(-n // ROWS)
    nt = ng * TILES
    last_base = n - ROWS
    kf = feat // P
    V, S, G, T, D = nc.vector, nc.scalar, nc.gpsimd, nc.tensor, nc.sync

    def dram(name, shape, dt=F32):
        return nc.dram_tensor(name, shape, dt, kind="Internal").ap()

    ctx = ExitStack()
    with ctx:
        def sb(name, shape, dt=F32):
            return ctx.enter_context(nc.sbuf_tensor(name, shape, dt))

        flow = Flow(nc, ctx)
        psum = ctx.enter_context(nc.psum_tensor("psum", [P, 4096], F32))

        def bank(first, count):
            return psum[:, first * 512:(first + count) * 512]

        link_recs = dram("link_recs", [links, 4])
        slot_dst = dram("slot_dst", [nt, P])
        slot_open = dram("slot_open", [nt, P])
        xw = dram("xw", [n, feat])
        hop_a = dram("hop_a", [n, feat])
        hop_b = dram("hop_b", [n, feat])
        x1 = dram("x1", [n, feat])
        x2 = dram("x2", [n, feat])
        x3 = dram("x3", [n, feat])
        tab1 = dram("tab1", [n, feat])
        recv1 = dram("recv1", [n, feat])
        heads1, cols1 = a["L1_gnn_W_s"].shape[1:]
        heads2, cols2 = a["L2_gnn_att_src"].shape
        heads3, cols3 = a["L3_gnn_att_src"].shape
        f2, f3 = heads2 * cols2, heads3 * cols3
        w2, w3 = f2 + 2 * heads2, f3 + 2 * heads3
        tab2 = dram("tab2", [n, w2])
        tab3 = dram("tab3", [n, w3])

        ident = sb("ident", [P, P])
        iota_row = sb("iota_row", [P, P])
        iota_col = sb("iota_col", [P, 1])
        ones = sb("ones", [P, P])
        base_row = sb("base_row", [P, nt])
        link_src = sb("link_src", [P, nt], I32)
        link_dst = sb("link_dst", [P, nt])
        link_end = sb("link_end", [P, nt])
        inv_deg = sb("inv_deg", [P, nt])
        no_link = sb("no_link", [P, nt])
        power = sb("power", [P, 2 * TILES])
        neg_slope = sb("neg_slope", [P, 1])

        weights = {}

        def weight(name, shape, src):
            weights[name] = (sb(name, shape), src)
            return weights[name][0]

        def chunks(w):
            return w.rearrange("(c p) m -> p c m", p=P)

        def spread(row, m):
            return row.rearrange("(o m) -> o m", o=1).to_broadcast([P, m])

        w_l0a = weight("w_l0a", [P, kf, feat], chunks(a["L0_gnn_W1"]))
        w_l0b = weight("w_l0b", [P, kf, feat], chunks(a["L0_gnn_W2"]))
        w_snd = weight("w_snd", [P, kf, feat], chunks(a["L1_gnn_W_s"].rearrange("d h k -> d (h k)")))
        w_rcv = weight("w_rcv", [P, kf, feat], chunks(a["L1_gnn_W_r"].rearrange("d h k -> d (h k)")))
        w_g2 = weight("w_g2", [P, kf, f2], chunks(a["L2_gnn_W"]))
        w_p2 = weight("w_p2", [P, feat], a["L2_gnn_Wp"])
        w_g3 = weight("w_g3", [P, kf, f3], chunks(a["L3_gnn_W"]))
        b_l0a = weight("b_l0a", [P, feat], spread(a["L0_gnn_b1"], feat))
        b_l0b = weight("b_l0b", [P, feat], spread(a["L0_gnn_b2"], feat))
        b_snd = weight("b_snd", [P, feat], spread(a["L1_gnn_b_s"].rearrange("h k -> (h k)"), feat))
        b_rcv = weight("b_rcv", [P, feat], spread(a["L1_gnn_b_r"].rearrange("h k -> (h k)"), feat))
        a_w = weight("a_w", [P, cols1], spread(a["L1_gnn_a_w"], cols1))
        a_b = weight("a_b", [P, 1], spread(a["L1_gnn_a_b"], 1))
        b_g2 = weight("b_g2", [P, f2], spread(a["L2_gnn_bias"], f2))
        b_p2 = weight("b_p2", [P, feat], spread(a["L2_gnn_bp"], feat))
        b_g3 = weight("b_g3", [P, f3], spread(a["L3_gnn_bias"], f3))
        slope = weight("slope", [P, 1], spread(a["L0_gnn_a"], 1))
        att2 = weight("att2", [P, 2, f2], None)
        att3 = weight("att3", [P, 2, f3], None)
        w_a2 = sb("w_a2", [P, kf, 2, heads2])
        w_a3 = sb("w_a3", [P, kf, 2, heads3])
        att_tmp = sb("att_tmp", [P, max(f2, f3)])

        s_w, s_c = flow.sem("weights"), flow.sem("const")

        def rows(t, q):
            r0 = min(q.g * ROWS, last_base) if q.static else None
            sl = slice(r0, r0 + ROWS) if q.static else bass.ds(q.g * ROWS, ROWS)
            return t[sl, :].rearrange("(k p) f -> p k f", p=P)

        def tiles(q, k=None):
            c0, m = (q.g * TILES, TILES) if k is None else (q.g * TILES + k, 1)
            return slice(c0, c0 + m) if q.static else bass.ds(c0, m)

        def split(t, par, width):
            return t[:, par, 0:TILES * width].rearrange("p (k w) -> p k w", k=TILES)

        HALF = TILES // 2

        def transpose_rows(ph, name, src, to, ps, after, ps_free, to_free, chunks_=kf):
            parts = 2 if chunks_ > 1 else 1
            m = TILES // parts
            for h in range(parts):
                def tr(q, h=h):
                    for k in range(m):
                        for c in range(chunks_):
                            o = (k * chunks_ + c) * P
                            i = T.transpose(ps[:, o:o + P], src(q)[:, h * m + k, c * P:(c + 1) * P], ident[:])
                    return i

                def cp(q, h=h):
                    w = m * chunks_ * P
                    return S.copy(to(q)[:, h * w:(h + 1) * w], ps[:, 0:w])
                ph.step("pe", f"{name}_tr{h}", after + (ps_free if h == 0 else [(f"{name}_xt0", 0)]), tr)
                ph.step("act", f"{name}_xt{h}", [(f"{name}_tr{h}", 0)] + (to_free if h == 0 else []), cp)

        def product(frm, w, width, ps, k0, k1, chunks_=kf):
            def mm(q):
                flat = frm(q)
                for k in range(k0, k1):
                    out_ = ps[:, (k - k0) * width:(k - k0 + 1) * width]
                    for c in range(chunks_):
                        o = (k * chunks_ + c) * P
                        i = T.matmul(out_, flat[:, o:o + P], w[:, c, :] if chunks_ > 1 else w[:],
                                     start=(c == 0), stop=(c == chunks_ - 1))
                return i
            return mm

        def grid(ps, width, m=TILES):
            return ps[:, 0:m * width].rearrange("p (k w) -> p k w", k=m)

        def bc(row, width, m=TILES):
            return row[:, 0:width].unsqueeze(1).to_broadcast([P, m, width])

        step_cols = 2 * STAGE
        raw = -(-e // P)
        ec = -(-raw // step_cols) * step_cols
        tail = e - (P - 1) * raw
        assert 2 < tail <= raw and n >= 2 * ROWS
        with ExitStack() as tmp:
            def tb(name, shape, dt=F32):
                return tmp.enter_context(nc.sbuf_tensor(name, shape, dt))
            src_i = tb("src_i", [P, raw], I32)
            near = [tb(f"dst_i{k}", [P, raw], I32) for k in range(4)]
            nearf = [tb(f"dst_f{k}", [P, raw]) for k in range(4)]
            edge_i = tb("edge_i", [P, raw], I32)
            edge_f = tb("edge_f", [P, raw])
            is_end = tb("is_end", [P, raw])
            recs = tb("recs", [P, ec, 4])
            pos = tb("pos", [P, ec], I32)
            base_i = tb("base_i", [P, nt], I32)
            below = tb("below", [P, 512])
            scratch = tb("scratch", [P, raw])
            first_link = tb("first_link", [P, nt])
            slot_idx = tb("slot_idx", [P, nt], I32)
            recs_t = tb("recs_t", [P, nt, 4])
            row_t = tb("row_t", [P, P])
            open_t = tb("open_t", [P, nt])
            in_tile = tb("in_tile", [P, nt])
            tmp_t = tb("tmp_t", [P, nt])
            pos_stage = tb("pos_stage", [P, 2, STAGE], I32)
            rec_stage = tb("rec_stage", [P, 2, STAGE, 4])
            iota_i = tb("iota_i", [P, P + 1], I32)

            pad_value = [-1, -1, -1, -1]
            s_e, s_pad, s_v = flow.sem("edges"), flow.sem("pad"), flow.sem("setup")
            with nc.Block() as block:
                chain = [0]

                def link(ins):
                    chain[0] += 1
                    ins.then_inc(s_v, 1)
                    V.wait_ge(s_v, chain[0])

                @block.sync
                def _(eng):
                    for handle, src in weights.values():
                        if src is not None:
                            eng.dma_start(handle[:], src).then_inc(s_w, 16)
                    for t, name in ((att2, "L2"), (att3, "L3")):
                        for j, side in enumerate(("src", "dst")):
                            v = a[f"{name}_gnn_att_{side}"].rearrange("h c -> (h c)")
                            eng.dma_start(t[:, j, :], spread(v, v.shape[0])).then_inc(s_w, 16)
                    eng.wait_ge(s_pad, 1)
                    for t, shift, src in [(src_i, 0, a["src"])] + [(near[k], k - 1, a["dst"]) for k in range(4)]:
                        head = max(0, -shift)
                        if head:
                            eng.dma_start(t[0:1, head:raw], src[0:raw - head].rearrange("(o m) -> o m", o=1)).then_inc(s_e, 16)
                            eng.dma_start(t[1:P - 1, :], src[raw - head:(P - 1) * raw - head].rearrange("(p m) -> p m", m=raw)).then_inc(s_e, 16)
                        else:
                            eng.dma_start(t[0:P - 1, :], src[shift:(P - 1) * raw + shift].rearrange("(p m) -> p m", m=raw)).then_inc(s_e, 16)
                        got = min(tail - shift, raw) if shift >= 0 else tail
                        eng.dma_start(t[P - 1:P, 0:got], src[(P - 1) * raw + shift:(P - 1) * raw + shift + got].rearrange("(o m) -> o m", o=1)).then_inc(s_e, 16)
                    eng.wait_ge(s_e, 11 * 16)
                    eng.wait_ge(s_w, 16 * (len(weights) - 2 + 4))

                @block.gpsimd
                def _(eng):
                    for k in range(4):
                        eng.memset(near[k][:], pad_value[k])
                    eng.memset(src_i[:], 0).then_inc(s_pad, 1)
                    eng.memset(ident[:], 0.0)
                    eng.memset(ones[:], 1.0)
                    eng.memset(recs[:], 0.0)
                    eng.memset(pos[:], int(FAR))
                    eng.memset(power[:, 0:TILES], -0.5)
                    eng.memset(power[:, TILES:2 * TILES], 0.5)
                    eng.memset(below[:], 0.0)
                    eng.memset(recs_t[:], -FAR).then_inc(s_pad, 1)
                    eng.iota(edge_i[:], [[1, raw]], base=0, channel_multiplier=raw)
                    full = nt - TILES
                    eng.iota(base_i[:, 0:full], [[P, full]], base=0, channel_multiplier=0)
                    eng.iota(base_i[:, full:nt], [[P, TILES]], base=last_base, channel_multiplier=0)
                    eng.iota(iota_i[:, 0:P], [[1, P]], base=0, channel_multiplier=0)
                    eng.iota(iota_i[:, P:P + 1], [[0, 1]], base=0, channel_multiplier=1).then_inc(s_c, 1)
                    eng.wait_ge(s_pad, 2)
                    eng.affine_select(out=ident[:], in_=ident[:], compare_op=ALU.not_equal, fill=1.0, base=0,
                                      pattern=[[-1, P]], channel_multiplier=1).then_inc(s_c, 1)

                @block.vector
                def _(eng):
                    eng.wait_ge(s_c, 2)
                    V.tensor_copy(iota_row[:], iota_i[:, 0:P])
                    V.tensor_copy(iota_col[:], iota_i[:, P:P + 1])
                    V.tensor_copy(base_row[:], base_i[:])
                    V.tensor_copy(edge_f[:], edge_i[:])
                    eng.wait_ge(s_e, 11 * 16)
                    for k in range(4):
                        V.tensor_copy(nearf[k][:], near[k][:])
                    link(V.tensor_copy(recs[:, 0:raw, 0], src_i[:]))
                    before, here, after, after2 = (t[:] for t in nearf)
                    V.tensor_copy(recs[:, 0:raw, 1], here)
                    V.tensor_tensor(is_end[:], here, after, ALU.not_equal)
                    V.tensor_tensor(edge_f[:], edge_f[:], here, ALU.subtract)
                    V.tensor_tensor(scratch[:], after, after2, ALU.is_equal)
                    link(V.tensor_tensor(recs[:, 0:raw, 3], before, here, ALU.not_equal))
                    link(V.tensor_scalar(scratch[:], scratch[:], -FAR, None, ALU.mult))
                    link(V.tensor_tensor(recs[:, 0:raw, 2], scratch[:], here, ALU.add))
                    link(V.scalar_tensor_tensor(scratch[:], is_end[:], FAR, edge_f[:], ALU.mult, ALU.add))
                    link(V.tensor_copy(pos[:, 0:raw], scratch[:]))
                    eng.wait_ge(s_w, 16 * (len(weights) - 2 + 4))
                    link(V.tensor_scalar(neg_slope[:], slope[:], -1.0, None, ALU.mult))
                    for w, att, wa, heads, width in ((w_g2, att2, w_a2, heads2, f2), (w_g3, att3, w_a3, heads3, f3)):
                        for c in range(kf):
                            for j in range(2):
                                link(V.tensor_tensor(att_tmp[:, 0:width], w[:, c, :], att[:, j, :], ALU.mult))
                                link(V.tensor_reduce(wa[:, c, j, :], att_tmp[:, 0:width].rearrange("p (h c) -> p h c", h=heads),
                                                     AX.X, ALU.add))

            rounds = ec // step_cols
            counts = -(-nt // rounds)
            assert counts * rounds <= 512 and nt <= 512
            s_cnt = flow.sem("count")
            s_stage, s_sent = flow.sem("stage"), [flow.sem("sent0"), flow.sem("sent1")]
            thr = tb("thr", [P, counts * rounds])
            first_sum = tb("first_sum", [P, nt])
            s_q, s_got = flow.sem("first"), [flow.sem("got0"), flow.sem("got1")]
            s_back = flow.sem("back")
            pads = P * raw - e
            full_rounds = nt // step_cols
            extra = -(-(nt - full_rounds * step_cols) // STAGE)
            got = tb("got", [P, 2, STAGE, 4])

            def links_vector(eng):
                V.memset(thr[:], 0.0).then_inc(s_pad, 1)
                eng.wait_ge(s_pad, 3)
                V.tensor_copy(thr[:, 0:nt], base_row[:]).then_inc(s_pad, 1)
                eng.wait_ge(s_pad, 4)

                def one_round(r, first):
                    for half in range(2):
                        if not first:
                            eng.wait_ge(s_sent[half], r * (16 * STAGE))
                        c0 = bass.ds(r * step_cols + half * STAGE, STAGE)
                        V.tensor_copy(pos_stage[:, half, :], pos[:, c0])
                        V.tensor_copy(rec_stage[:, half, :, :], recs[:, c0, :]).then_inc(s_stage, 1)
                    for k in range(counts):
                        t = bass.ds(r * counts + k, 1)
                        V.tensor_scalar(scratch[:], nearf[1][:], thr[:, t], 0.0, ALU.is_lt, ALU.add,
                                        accum_out=below[:, t]).then_inc(s_cnt, 1)
                        eng.wait_ge(s_cnt, r * counts + k + 1)

                one_round(0, True)
                with eng.Fori(1, rounds) as r:
                    one_round(r, False)
                link(V.memset(got[:], -FAR))
                eng.wait_ge(s_q, 1)
                link(V.tensor_tensor(first_link[:], first_sum[:], base_row[:], ALU.subtract))
                link(V.tensor_scalar(first_link[:], first_link[:], iota_col[:, 0:1], float(-pads), ALU.add, ALU.add))
                V.tensor_copy(slot_idx[:], first_link[:]).then_inc(s_q, 1)
                eng.wait_ge(s_q, 2)

                def stage(b, half):
                    V.tensor_copy(pos_stage[:, half, :], slot_idx[:, bass.ds(b, STAGE)]).then_inc(s_stage, 1)

                def take(b, half, r):
                    eng.wait_ge(s_got[half], (r + 1) * (16 * STAGE))
                    V.tensor_copy(recs_t[:, bass.ds(b, STAGE), :], got[:, half, :, :]).then_inc(s_back, 1)

                with eng.Fori(0, full_rounds) as r:
                    for half in range(2):
                        stage(r * step_cols + half * STAGE, half)
                    for half in range(2):
                        take(r * step_cols + half * STAGE, half, r)
                for half in range(extra):
                    b = min(full_rounds * step_cols + half * STAGE, nt - STAGE)
                    stage(b, half)
                    take(b, half, full_rounds)
                eng.wait_ge(s_back, 2 * full_rounds + extra)
                V.tensor_tensor(link_end[:], recs_t[:, :, 2], base_row[:], ALU.subtract)
                V.tensor_scalar(open_t[:], recs_t[:, :, 3], -BIG, None, ALU.mult)
                link(V.tensor_tensor(link_dst[:], recs_t[:, :, 1], base_row[:], ALU.subtract))
                V.tensor_scalar(in_tile[:], link_dst[:], -0.5, None, ALU.is_gt)
                link(V.tensor_scalar(tmp_t[:], link_dst[:], P - 0.5, None, ALU.is_lt))
                link(V.tensor_tensor(in_tile[:], in_tile[:], tmp_t[:], ALU.mult))
                link(V.tensor_scalar(tmp_t[:], in_tile[:], -FAR, FAR, ALU.mult, ALU.add))
                link(V.tensor_tensor(tmp_t[:], tmp_t[:], recs_t[:, :, 0], ALU.add))
                V.tensor_scalar(tmp_t[:], tmp_t[:], 0.0, None, ALU.max).then_inc(s_q, 1)
                eng.wait_ge(s_q, 3)
                V.tensor_copy(link_src[:], tmp_t[:]).then_inc(s_q, 1)

            def links_gpsimd(eng):
                with eng.Fori(0, rounds) as r:
                    for half in range(2):
                        eng.wait_ge(s_stage, r * 2 + half + 1)
                        eng.sem_inc(flow.sem("passed"), 1)
                        for k in range(STAGE):
                            eng.indirect_dma_start(
                                out=link_recs, out_offset=bass.IndirectOffsetOnAxis(ap=pos_stage[:, half, k:k + 1], axis=0),
                                in_=rec_stage[:, half, k, :], in_offset=None,
                                bounds_check=links - 1, oob_is_err=False).then_inc(s_sent[half], 16)
                for half in range(2):
                    eng.wait_ge(s_sent[half], rounds * 16 * STAGE)
                eng.wait_ge(s_cnt, rounds * counts)
                eng.partition_all_reduce(first_sum[:], below[:, 0:nt], P, bass.bass_isa.ReduceOp.add).then_inc(s_q, 1)

                def fetch(half, seq):
                    eng.wait_ge(s_stage, 2 * rounds + seq + 1)
                    eng.sem_inc(flow.sem("passed"), 1)
                    for k in range(STAGE):
                        eng.indirect_dma_start(
                            out=got[:, half, k, :], out_offset=None, in_=link_recs,
                            in_offset=bass.IndirectOffsetOnAxis(ap=pos_stage[:, half, k:k + 1], axis=0),
                            bounds_check=links - 1, oob_is_err=False).then_inc(s_got[half], 16)
                eng.wait_ge(s_q, 2)
                with eng.Fori(0, full_rounds) as r:
                    for half in range(2):
                        fetch(half, r * 2 + half)
                for x in range(extra):
                    fetch(x, full_rounds * 2 + x)
                for half in range(2):
                    eng.wait_ge(s_got[half], (full_rounds + (1 if half < extra else 0)) * 16 * STAGE)

            ph = Phase(flow, ng)
            x_in = tb("x_in", [P, 3, TILES, feat])
            x_t = tb("x_t", [P, 2, TILES * feat])
            x_o = tb("x_o", [P, 2, TILES, feat])
            ph.dma("sp", "own_x", [("up_tr1", 3)], lambda q: [D.dma_start(x_in[:, q.tri], rows(a["x"], q))], depth=3)
            transpose_rows(ph, "up", lambda q: x_in[:, q.tri], lambda q: x_t[:, q.par], bank(0, 1), [("own_x", 0)], [("up_xt1", 1)], [("up_mm", 2)])
            ph.at(1)
            ph.step("pe", "up_mm", [("up_xt1", 0), ("mean", 1)], product(lambda q: x_t[:, q.par], w_l0a, feat, bank(2, 2), 0, TILES))
            ph.at(1, 4)
            ph.step("act", "mean", [("up_mm", 0), ("st_a", 2)], lambda q: S.copy(x_o[:, q.par], grid(bank(2, 2), feat)))
            ph.dma("act", "st_a", [("mean", 0)], lambda q: [S.dma_start(rows(xw, q), x_o[:, q.par])])
            ph.run(nc, besides={"dve": links_vector, "pool": links_gpsimd})

            nb = -(-nt // P)
            bt = nt // nb if nt % nb == 0 else None
            assert bt is not None
            s_tr, s_tc, s_ts = flow.sem("row_tr"), flow.sem("row_cp"), flow.sem("row_st")
            with nc.Block() as block:
                @block.tensor
                def _(eng):
                    for i in range(2 * nb):
                        t = (link_dst, open_t)[i // nb]
                        b = i % nb
                        eng.wait_ge(s_tc, i)
                        T.transpose(bank(0, 1)[0:bt, 0:P], t[:, b * bt:(b + 1) * bt], ident[:]).then_inc(s_tr, 1)

                @block.vector
                def _(eng):
                    for i in range(2 * nb):
                        eng.wait_ge(s_tr, i + 1)
                        eng.wait_ge(s_ts, 16 * i)
                        V.tensor_copy(row_t[0:bt, :], bank(0, 1)[0:bt, 0:P]).then_inc(s_tc, 1)

                @block.sync
                def _(eng):
                    for i in range(2 * nb):
                        d = (slot_dst, slot_open)[i // nb]
                        b = i % nb
                        eng.wait_ge(s_tc, i + 1)
                        eng.dma_start(d[b * bt:(b + 1) * bt, :], row_t[0:bt, :]).then_inc(s_ts, 16)
                    eng.wait_ge(s_ts, 16 * 2 * nb)

        wide = max(feat, w2, w3)
        own_x = sb("own_x", [P, 3, TILES, feat])
        own_t = sb("own_t", [P, RING, TILES * wide])
        got_rows = sb("got_rows", [P, RING, TILES * wide])
        idx = sb("idx", [P, RING, TILES], I32)
        sel = sb("sel", [P, RING, TILES, P])
        sel_end = sb("sel_end", [P, 3, TILES, P])
        sel_t = sb("sel_t", [P, RING, TILES, P])
        own_r = sb("own_r", [P, 2, TILES, feat])
        dst_rows = sb("dst_rows", [P, 2, TILES * P])
        opens = sb("opens", [TILES * heads1, 2, P])
        xt = sb("xt", [P, 2, TILES * feat])
        t0 = sb("t0", [P, TILES, feat])
        t1 = sb("t1", [P, TILES, feat])
        t2 = sb("t2", [P, TILES, feat])
        t3 = sb("t3", [P, TILES, feat])
        z = sb("z", [P, 2 * TILES, feat])
        zv = sb("zv", [P, 2 * TILES, feat])
        res = sb("res", [P, 2, TILES, feat])
        tab_o = sb("tab_o", [P, 2, TILES * wide])
        stats = sb("stats", [P, TILES, 6])
        moments = sb("moments", [P, TILES, 5])
        var_eps = sb("var_eps", [P, TILES])
        rstd = sb("rstd", [P, TILES])
        shift = sb("shift", [P, TILES])
        deg = sb("deg", [P, TILES])
        sq = sb("sq", [P, TILES])
        norm_v = sb("norm_v", [P, 3, TILES])
        scanned = sb("scanned", [P, 2, P])

        s_init = flow.sem("init")
        with nc.Block() as block:
            @block.gpsimd
            def _(eng):
                eng.memset(got_rows[:], 0.0).then_inc(s_init, 1)
                eng.memset(scanned[:], 0.0).then_inc(s_init, 1)
                eng.wait_ge(s_init, 2)

        def fetch_links(ph, table, width, done, sel_done):
            ph.step("dve", "idx", [("gather", 6)], lambda q: V.tensor_copy(idx[:, q.slot, :], link_src[:, tiles(q)]))
            ph.dma("pool", "gather", [("idx", 0), (done, 6)], lambda q: [
                G.indirect_dma_start(out=got_rows[:, q.slot, k * width:(k + 1) * width], out_offset=None, in_=table,
                                     in_offset=bass.IndirectOffsetOnAxis(ap=idx[:, q.slot, k:k + 1], axis=0),
                                     bounds_check=n - 1, oob_is_err=False) for k in range(TILES)], count=TILES, depth=RING)
            ph.step("dve", "sel", [(sel_done, 6)], lambda q: V.tensor_tensor(
                sel[:, q.slot], iota_row[:].unsqueeze(1).to_broadcast([P, TILES, P]),
                link_dst[:, tiles(q)].unsqueeze(2).to_broadcast([P, TILES, P]), ALU.is_equal))

        def layer_norm(ph, src, after, dst, dst_free):
            def st(q):
                for k in range(TILES):
                    i = V.bn_stats(stats[:, k, :], src(q)[:, k, :])
                return i

            def halves(q):
                V.tensor_tensor(moments[:, :, 0], stats[:, :, 1], stats[:, :, 4], ALU.add)
                V.tensor_tensor(moments[:, :, 1], stats[:, :, 1], stats[:, :, 4], ALU.subtract)
                return V.tensor_tensor(moments[:, :, 2], stats[:, :, 2], stats[:, :, 5], ALU.add)

            def parts(q):
                V.tensor_scalar(moments[:, :, 3], moments[:, :, 2], 1.0 / feat, EPS, ALU.mult, ALU.add)
                return V.scalar_tensor_tensor(moments[:, :, 4], moments[:, :, 1], 0.25, moments[:, :, 1], ALU.mult, ALU.mult)

            def ln(q):
                for k in range(TILES):
                    i = S.activation(dst(q)[:, k, :], src(q)[:, k, :], ACT.Identity, bias=shift[:, k:k + 1], scale=rstd[:, k:k + 1])
                return i
            ph.step("dve", "stats", after + [("halves", 1)], st)
            ph.step("dve", "halves", [("stats", 0), ("parts", 1), ("shift", 1)], halves)
            ph.step("dve", "parts", [("halves", 0), ("veps", 1)], parts)
            ph.step("dve", "veps", [("parts", 0), ("rstd", 1)], lambda q: V.tensor_tensor(var_eps[:], moments[:, :, 3], moments[:, :, 4], ALU.add))
            ph.step("pool", "rstd", [("veps", 0), ("ln", 1)], lambda q: G.tensor_tensor(rstd[:], var_eps[:], power[:, 0:TILES], ALU.pow))
            ph.step("dve", "shift", [("rstd", 0)], lambda q: V.scalar_tensor_tensor(
                shift[:], moments[:, :, 0], -0.5, rstd[:], ALU.mult, ALU.mult))
            ph.step("act", "ln", [("shift", 0)] + dst_free, ln)

        def hop(table, kind, outs, first=False):
            ph = Phase(flow, ng, ORDER[("first" if first else kind)])
            agg = [bank(0, 2), bank(2, 2)] if kind != "x1" else [bank(0, 2), bank(0, 2)]
            tp, dn = bank(4, 1) if kind == "h1" else bank(2, 1), bank(6, 2) if kind == "h1" else bank(4, 2)
            deg_ps = bank(5, 1)
            sums = own_r
            ph.dma("sp", "own_t", [("sums", 6)], lambda q: [D.dma_start(split(own_t, q.slot, feat), rows(table, q))], depth=RING)
            if kind == "x1":
                ph.dma("sp", "own_x", [("add_x", 3)], lambda q: [D.dma_start(own_x[:, q.tri], rows(a["x"], q))], depth=3)
            fetch_links(ph, table, feat, "agg", "agg")


            def sum_links(q):
                g = split(got_rows, q.slot, feat)
                for k in range(TILES):
                    i = T.matmul(agg[q.par][:, k * feat:(k + 1) * feat], sel[:, q.slot, k, :], g[:, k, :], start=True, stop=True)
                    if first:
                        i = T.matmul(deg_ps[:, k:k + 1], sel[:, q.slot, k, :], ones[:, 0:1], start=True, stop=True)
                return i
            ph.step("pe", "agg", [("gather", 0), ("sel", 0), ("sums", 1 if kind == "x1" else 2)] + ([("deg", 1), ("no_link", 1)] if first else []), sum_links)
            if first:
                ph.step("dve", "deg", [("agg", 0), ("inv", 1)], lambda q: V.tensor_scalar(deg[:], deg_ps[:, 0:TILES], 1.0, None, ALU.add))
                ph.step("dve", "no_link", [("deg", 0)], lambda q: V.tensor_scalar(
                    no_link[:, tiles(q)], deg_ps[:, 0:TILES], 0.5, -BIG, ALU.is_lt, ALU.mult))
                ph.step("dve", "inv", [("deg", 0)], lambda q: V.reciprocal(inv_deg[:, tiles(q)], deg[:]))
            sums_free = {"hop": ("mean", 2), "h1": ("biased", 2), "x1": ("pre_b", 2)}[kind]
            ph.step("dve", "sums", [("agg", 0), ("own_t", 0), sums_free], lambda q: V.tensor_tensor(
                sums[:, q.par], grid(agg[q.par], feat), split(own_t, q.slot, feat), ALU.add))
            if kind == "hop":
                def mean(q):
                    for k in range(TILES):
                        i = S.mul(res[:, q.par, k, :], sums[:, q.par, k, :], inv_deg[:, tiles(q, k)])
                    return i
                ph.step("act", "mean", [("sums", 0), ("st_a", 2)] + ([("inv", 0)] if first else []), mean)
                ph.dma("act", "st_a", [("mean", 0)], lambda q: [S.dma_start(rows(outs[0], q), res[:, q.par])])
                ph.run(nc)
                return

            b = b_l0a if kind == "h1" else b_l0b

            def mean_bias(q):
                for k in range(TILES):
                    i = V.scalar_tensor_tensor(t0[:, k, :], sums[:, q.par, k, :], inv_deg[:, tiles(q, k)], b[:], ALU.mult, ALU.add)
                return i
            if kind == "x1":
                ph.step("dve", "pre_b", [("sums", 0), ("pos", 1), ("neg", 1)], mean_bias)
                ph.step("dve", "biased", [("pre_b", 0), ("own_x", 0)], lambda q: V.tensor_tensor(t0[:], t0[:], own_x[:, q.tri], ALU.add))
            else:
                ph.step("dve", "biased", [("sums", 0), ("pos", 1), ("neg", 1)], mean_bias)
            ph.step("act", "pos", [("biased", 0), ("prelu", 1)], lambda q: S.activation(t1[:], t0[:], ACT.Relu))
            ph.step("act", "neg", [("biased", 0), ("prelu", 1)], lambda q: S.activation(t2[:], t0[:], ACT.Relu, scale=-1.0))
            if kind == "h1":
                ph.step("dve", "prelu", [("pos", 0), ("neg", 0), ("up_tr1", 2)], lambda q: V.scalar_tensor_tensor(
                    res[:, q.par], t2[:], neg_slope[:, 0:1], t1[:], ALU.mult, ALU.add))
                xt_of = lambda q: xt[:, q.par]
                transpose_rows(ph, "up", lambda q: res[:, q.par], xt_of, tp, [("prelu", 0)], [("up_xt1", 1)], [("up_mm", 2)])
                ph.step("pe", "up_mm", [("up_xt1", 0), ("mean", 1)], product(xt_of, w_l0b, feat, dn, 0, TILES))
                tab4 = lambda q: split(tab_o, q.par, feat)
                ph.step("act", "mean", [("up_mm", 0), ("st_a", 2)], lambda q: S.copy(tab4(q), grid(dn, feat)))
                ph.dma("act", "st_a", [("mean", 0)], lambda q: [S.dma_start(rows(outs[0], q), tab4(q))])
                ph.run(nc)
                return
            ph.step("dve", "prelu", [("pos", 0), ("neg", 0), ("ln", 1)], lambda q: V.scalar_tensor_tensor(
                t3[:], t2[:], neg_slope[:, 0:1], t1[:], ALU.mult, ALU.add))
            ph.step("pool", "add_x", [("prelu", 0)], lambda q: G.tensor_tensor(t3[:], t3[:], own_x[:, q.tri], ALU.add))
            layer_norm(ph, lambda q: t3, [("add_x", 0)], lambda q: res[:, q.par], [("st_a", 2), ("x1_tr1", 2)])
            ph.dma("act", "st_a", [("ln", 0)], lambda q: [S.dma_start(rows(outs[0], q), res[:, q.par])])
            zt = lambda q: z[:, q.par * TILES:(q.par + 1) * TILES, :].rearrange("p k f -> p (k f)")
            zr = lambda q: zv[:, q.par * TILES:(q.par + 1) * TILES, :]
            snd_ps, rcv_ps = bank(4, 2), bank(6, 2)
            transpose_rows(ph, "x1", lambda q: res[:, q.par], zt, tp, [("ln", 0)], [("x1_xt1", 1)], [("snd_mm", 2), ("rcv_mm", 2)])
            ph.step("pe", "snd_mm", [("x1_xt1", 0), ("snd", 1)], product(zt, w_snd, feat, snd_ps, 0, TILES))
            ph.step("pe", "rcv_mm", [("x1_xt1", 0), ("rcv", 1)], product(zt, w_rcv, feat, rcv_ps, 0, TILES))
            ph.step("dve", "snd", [("snd_mm", 0), ("st_s", 2)], lambda q: V.tensor_tensor(split(tab_o, q.par, feat), grid(snd_ps, feat), bc(b_snd, feat), ALU.add))
            ph.dma("act", "st_s", [("snd", 0)], lambda q: [S.dma_start(rows(outs[1], q), split(tab_o, q.par, feat))])
            ph.step("dve", "rcv", [("rcv_mm", 0), ("st_r", 2)], lambda q: V.tensor_tensor(zr(q), grid(rcv_ps, feat), bc(b_rcv, feat), ALU.add))
            ph.dma("act", "st_r", [("rcv", 0)], lambda q: [S.dma_start(rows(outs[2], q), zr(q))])
            ph.run(nc)

        small_names = ("maxes", "mx", "d_self", "d_link", "den", "inv", "w_link", "w_self")
        gat_small = {k: sb("g_" + k, [P, TILES, heads1]) for k in small_names}
        p_self = sb("p_self", [P, 2, TILES, heads1])
        p_link = sb("p_link", [P, 2, TILES, heads1])
        logits = sb("logits", [P, 3, 2 * TILES, heads1])
        flat_logits = {h: sb(f"flat_logits{h}", [P, TILES * h]) for h in {heads1, heads2, heads3}}

        def gat(xin, table, width, heads, cols, loops, finish, v2=False):
            ph = Phase(flow, ng, ORDER[finish])
            TA = 8 if finish == "project" else 7
            x_done = {"x2": "agg", "project": "out_x", "out": "x_read"}[finish]
            f = heads * cols
            hk = TILES * heads
            agg_ps, spread_ps, sum_ps, tp, dn, log_ps, max_ps = (
                bank(0, 2), bank(2, 1), bank(3, 1), bank(4, 1), bank(5, 1), bank(6, 1), bank(7, 1))
            if finish == "project":
                agg_ps, o_ps = bank(0, 1), bank(1, 1)

            def field(ps, i):
                return ps[:, P + i * 64:P + i * 64 + hk].rearrange("p (k h) -> p k h", k=TILES)
            tmp = {k: v[:, :, 0:heads] for k, v in gat_small.items()}
            ps_ = lambda q: p_self[:, q.par, :, 0:heads]
            pl_ = lambda q: p_link[:, q.par, :, 0:heads]
            le = lambda q: logits[:, q.tri, 0:TILES, 0:heads]
            ls = lambda q: logits[:, q.tri, TILES:2 * TILES, 0:heads]
            lflat = flat_logits[heads]

            def slot_rows(t, q):
                c0 = q.g * TILES
                return t[slice(c0, c0 + TILES) if q.static else bass.ds(c0, TILES), :]
            ph.dma("sp", "own_t", [("v_self", 6)], lambda q: [D.dma_start(split(own_t, q.slot, width), rows(table, q))], depth=RING)
            if v2:
                ph.dma("sp", "own_r", [("z_self", 2), ("spread_r1", 2)], lambda q: [D.dma_start(own_r[:, q.par], rows(recv1, q))])
            ph.dma("sp", "dst_row", [("sel_t", 2)], lambda q: [D.dma_start(
                dst_rows[:, q.par, :], slot_rows(slot_dst, q).rearrange("(o k) s -> o (k s)", o=1).to_broadcast([P, TILES * P]))])
            ph.dma("sp", "open_row", [("scan", 2)], lambda q: [D.dma_start(
                opens[k * heads:(k + 1) * heads, q.par, :], slot_rows(slot_open, q)[k:k + 1, :].to_broadcast([heads, P])) for k in range(TILES)], count=TILES)
            ph.dma("sp", "own_x", [(x_done, 3)], lambda q: [D.dma_start(own_x[:, q.tri], rows(xin, q))], depth=3)
            fetch_links(ph, table, width, "v_link", "agg")
            ph.step("dve", "sel_t", [("dst_row", 0), ("agg", 6)], lambda q: V.tensor_scalar(
                sel_t[:, q.slot].rearrange("p k s -> p (k s)"), dst_rows[:, q.par, :], iota_col[:, 0:1], None, ALU.is_equal))
            ph.step("dve", "sel_end", [("seg_max", 3)], lambda q: V.tensor_tensor(
                sel_end[:, q.tri], iota_row[:].unsqueeze(1).to_broadcast([P, TILES, P]),
                link_end[:, tiles(q)].unsqueeze(2).to_broadcast([P, TILES, P]), ALU.is_equal))

            def each(out, lhs, rhs, k0=0, k1=TILES):
                def go(q):
                    at = q.tri if lhs is sel_end else q.slot
                    for k in range(k0, k1):
                        i = T.matmul(out(q)[:, k - k0, :], lhs[:, at, k, :], rhs(q)[:, k, :], start=True, stop=True)
                    return i
                return go

            if v2:
                z3 = z[:].rearrange("p k (h c) -> p (k h) c", c=cols)
                ph.step("pool", "z_self", [("own_r", 0), ("own_t", 0), ("z_sum", 1)], lambda q: G.tensor_tensor(
                    z[:, TILES:2 * TILES, :], split(own_t, q.slot, feat), own_r[:, q.par], ALU.add))
                for h in range(2):
                    ph.step("pe", f"spread_r{h}", [("own_r", 0), ("sel_t", 0), ("z_link0", 0) if h else ("z_link1", 1)],
                            each(lambda q: grid(spread_ps, feat, HALF), sel_t, lambda q: own_r[:, q.par], h * HALF, (h + 1) * HALF))
                    ph.step("dve", f"z_link{h}", [(f"spread_r{h}", 0), ("gather", 0), ("z_sum", 1)], lambda q, h=h: V.tensor_tensor(
                        z[:, h * HALF:(h + 1) * HALF, :], grid(spread_ps, feat, HALF),
                        split(got_rows, q.slot, feat)[:, h * HALF:(h + 1) * HALF, :], ALU.add))
                for side, after in (("link", "z_link1"), ("own", "z_self")):
                    half = z[:, 0:TILES, :] if side == "link" else z[:, TILES:2 * TILES, :]
                    up, down = (t0, t1) if side == "link" else (t2, t3)
                    ph.step("act", f"up_{side}", [(after, 0), (f"leaky_{side}", 1)], lambda q, o=up, i=half: S.activation(o[:], i, ACT.Relu))
                    ph.step("act", f"down_{side}", [(after, 0), (f"leaky_{side}", 1)], lambda q, o=down, i=half: S.activation(o[:], i, ACT.Relu, scale=-0.01))
                    ph.step("pool", f"leaky_{side}", [(f"up_{side}", 0), (f"down_{side}", 0)], lambda q, o=half, u=up, d=down: G.tensor_tensor(
                        o, u[:], d[:], ALU.subtract))
                ph.step("dve", "z_w", [("leaky_link", 0), ("leaky_own", 0)], lambda q: V.tensor_tensor(
                    z3, z3, a_w[:].unsqueeze(1).to_broadcast([P, 2 * TILES * heads, cols]), ALU.mult))
                ph.step("dve", "z_sum", [("z_w", 0), ("d_self", 3), ("d_link0", 3)], lambda q: V.tensor_reduce(
                    logits[:, q.tri].rearrange("p k h -> p (k h)"), z3, AX.X, ALU.add))
                ph.step("dve", "logit", [("z_sum", 0)], lambda q: V.tensor_scalar(
                    logits[:, q.tri], logits[:, q.tri], a_b[:, 0:1], None, ALU.add))
            else:
                ph.step("pe", "spread_a", [("own_t", 0), ("sel_t", 0), ("s_back", 2)] + ([] if finish == "out" else [("t_a", TA)]), each(
                    lambda q: field(log_ps, 0), sel_t, lambda q: split(own_t, q.slot, width)[:, :, f + heads:f + 2 * heads]))
                ph.step("dve", "z_self", [("own_t", 0), ("d_self", 3)], lambda q: V.tensor_tensor(
                    ls(q), split(own_t, q.slot, width)[:, :, f:f + heads], split(own_t, q.slot, width)[:, :, f + heads:f + 2 * heads], ALU.add))
                ph.step("dve", "z_link", [("spread_a", 0), ("gather", 0), ("d_link0", 3)], lambda q: V.tensor_tensor(
                    le(q), field(log_ps, 0), split(got_rows, q.slot, width)[:, :, f:f + heads], ALU.add))
                lg = lambda q: logits[:, q.tri, :, 0:heads]
                ph.step("dve", "logit", [("z_link", 0), ("z_self", 0)], lambda q: V.scalar_tensor_tensor(
                    lg(q), lg(q), 0.2, lg(q), ALU.mult, ALU.max))
            ph.step("dve", "l_flat", [("logit", 0), ("l_tr", 1)], lambda q: V.tensor_copy(lflat[:].rearrange("p (k h) -> p k h", k=TILES), le(q)))
            ph.step("pe", "l_tr", [("l_flat", 0), ("s_back", 1)] + ([("t_a", TA - 1)] if v2 else [("z_link", -1)]), lambda q: T.transpose(log_ps[0:hk, 0:P], lflat[:], ident[:]))
            ph.step("dve", "scan", [("l_tr", 0), ("open_row", 0), ("s_tr", 2)], lambda q: V.tensor_tensor_scan(
                scanned[0:hk, q.par, :], opens[0:hk, q.par, :], log_ps[0:hk, 0:P], -BIG, ALU.add, ALU.max))
            ph.step("pe", "s_tr", [("scan", 0)], lambda q: T.matmul(
                log_ps[:, 384:384 + hk], scanned[:, q.par, :], ident[:, 0:hk], start=True, stop=True))
            ph.step("act", "s_back", [("s_tr", 0), ("seg_max", 1)], lambda q: S.copy(
                tmp["maxes"], log_ps[:, 384:384 + hk].rearrange("p (k h) -> p k h", k=TILES)))

            ph.step("pe", "seg_max", [("s_back", 0), ("sel_end", 0), ("d_link0", 1)], each(lambda q: field(max_ps, 1), sel_end, lambda q: tmp["maxes"]))
            ph.step("dve", "mx0", [("seg_max", 0), ("spread_m", 1), ("d_self", 1)], lambda q: V.tensor_tensor(
                tmp["mx"], field(max_ps, 1), no_link[:, tiles(q)].unsqueeze(2).to_broadcast([P, TILES, heads]), ALU.add))
            ph.step("dve", "mx", [("mx0", 0)], lambda q: V.tensor_tensor(tmp["mx"], tmp["mx"], ls(q), ALU.max))
            ph.step("pe", "spread_m", [("mx", 0)], each(lambda q: field(max_ps, 2), sel_t, lambda q: tmp["mx"]))
            ph.step("dve", "d_self", [("mx", 0), ("p_self", 1)], lambda q: V.tensor_tensor(tmp["d_self"], ls(q), tmp["mx"], ALU.subtract))
            ph.step("act", "p_self", [("d_self", 0), ("w_self", 2)], lambda q: S.activation(ps_(q), tmp["d_self"], ACT.Exp))
            ph.step("dve", "d_link0", [("spread_m", 0), ("p_link", 1)], lambda q: V.tensor_tensor(tmp["d_link"], le(q), field(max_ps, 2), ALU.subtract))
            ph.step("dve", "d_link", [("d_link0", 0)], lambda q: V.tensor_scalar(tmp["d_link"], tmp["d_link"], 0.0, None, ALU.min))
            ph.step("act", "p_link", [("d_link", 0), ("w_link", 2), ("sum_p", 2)], lambda q: S.activation(pl_(q), tmp["d_link"], ACT.Exp))

            ph.step("pe", "sum_p", [("p_link", 0), ("sel", 0), ("w_link", 1)], each(lambda q: field(sum_ps, 0), sel, pl_))
            ph.step("dve", "den0", [("sum_p", 0), ("p_self", 0), ("inv_d", 1)], lambda q: V.scalar_tensor_tensor(
                tmp["den"], ps_(q), float(loops), field(sum_ps, 0), ALU.mult, ALU.add))
            ph.step("dve", "den", [("den0", 0)], lambda q: V.tensor_scalar(tmp["den"], tmp["den"], 1e-16 if finish == "project" else 0.0, None, ALU.add))
            ph.step("dve", "inv_d", [("den", 0), ("spread_i", 1), ("w_self", 1)], lambda q: V.reciprocal(tmp["inv"], tmp["den"]))
            ph.step("pe", "spread_i", [("inv_d", 0)], each(lambda q: field(sum_ps, 1), sel_t, lambda q: tmp["inv"]))
            ph.step("dve", "w_self", [("inv_d", 0), ("v_self", 1)], lambda q: V.scalar_tensor_tensor(
                tmp["w_self"], ps_(q), float(loops), tmp["inv"], ALU.mult, ALU.mult))
            ph.step("dve", "w_link", [("spread_i", 0), ("v_link", 1)], lambda q: V.tensor_tensor(tmp["w_link"], pl_(q), field(sum_ps, 1), ALU.mult))
            zl = zv[:, 0:TILES, 0:f]
            zs = zv[:, TILES:2 * TILES, 0:f]

            def heads4(v):
                return v.rearrange("p k (h c) -> p k h c", c=cols)
            ph.step("pool", "v_self", [("w_self", 0), ("agg", 1)], lambda q: G.tensor_tensor(
                heads4(zs), heads4(split(own_t, q.slot, width)[:, :, 0:f]),
                tmp["w_self"].unsqueeze(3).to_broadcast([P, TILES, heads, cols]), ALU.mult))
            ph.step("dve", "v_link", [("w_link", 0), ("agg", 1)], lambda q: V.tensor_tensor(
                heads4(zl), heads4(split(got_rows, q.slot, width)[:, :, 0:f]),
                tmp["w_link"].unsqueeze(3).to_broadcast([P, TILES, heads, cols]), ALU.mult))


            def agg(q):
                for k in range(TILES):
                    o = agg_ps[:, k * f:(k + 1) * f]
                    T.matmul(o, sel[:, q.slot, k, :], zl[:, k, :], start=True, stop=False)
                    i = T.matmul(o, ident[:], zs[:, k, :], start=False, stop=not v2)
                    if v2:
                        i = T.matmul(o, ident[:], own_x[:, q.tri, k, :], start=False, stop=True)
                return i
            ph.step("pe", "agg", [("v_self", 0), ("v_link", 0)] + ([("own_x", 0), ("ln", 1)] if v2 else [("out_b", 1)]), agg)
            agg_v = grid(agg_ps, f)

            def table_out(nxt_w, nxt_wa, nf, nheads, nwidth, dst, xsrc):
                o = lambda q: split(tab_o, q.par, nwidth)
                x_t = lambda q: xt[:, 0]
                transpose_rows(ph, "t", xsrc, x_t, tp, [("ln", 0)], [("t_xt1", 1)], [("t_mm", 1), (f"t_mm{TILES * nf // 512 - 1}", 1)])
                parts = TILES * nf // 512
                m = TILES // parts
                for h in range(parts):
                    ph.step("pe", f"t_mm{h}", [("t_xt1", 0), (f"t_h{h - 1}", 0) if h else (f"t_h{parts - 1}", 1)],
                            product(x_t, nxt_w, nf, dn, h * m, (h + 1) * m))
                    ph.step("act", f"t_h{h}", [(f"t_mm{h}", 0), ("st_t", 2)], lambda q, h=h: S.copy(
                        o(q)[:, h * m:(h + 1) * m, 0:nf], grid(dn, nf, m)))
                att = log_ps[:, 0:TILES * 2 * nheads]

                def mm(q):
                    for k in range(TILES):
                        for c in range(kf):
                            i = T.matmul(att[:, k * 2 * nheads:(k + 1) * 2 * nheads], xt[:, 0, (k * kf + c) * P:(k * kf + c + 1) * P],
                                         nxt_wa[:, c].rearrange("p j h -> p (j h)"), start=(c == 0), stop=(c == kf - 1))
                    return i
                ph.step("pe", "t_mm", [("t_xt1", 0), ("s_back", 2 - TA)], mm)
                ph.step("act", "t_a", [("t_mm", 0), ("st_t", 2)], lambda q: S.copy(
                    o(q)[:, :, nf:nwidth], att.rearrange("p (k w) -> p k w", k=TILES)))
                ph.dma("act", "st_t", [(f"t_h{parts - 1}", 0), ("t_a", 0)], lambda q: [S.dma_start(rows(dst, q), o(q))])

            if finish == "x2":
                layer_norm(ph, lambda q: agg_v, [("agg", 0)], lambda q: res[:, q.par], [("st_a", 2), ("t_tr1", 2)])
                ph.dma("act", "st_a", [("ln", 0)], lambda q: [S.dma_start(rows(x2, q), res[:, q.par])])
                table_out(w_g2, w_a2, f2, heads2, w2, tab2, lambda q: res[:, q.par])
            elif finish == "project":
                ph.step("dve", "out_b", [("agg", 0), ("o_tr0", 1)], lambda q: V.tensor_tensor(t0[:, :, 0:f], agg_v, bc(b_g2, f), ALU.add))
                o_t = lambda q: xt[:, 1]
                t13 = lambda q: (t1, t3)[q.par]
                transpose_rows(ph, "o", lambda q: t0, o_t, o_ps, [("out_b", 0)], [("o_xt0", 1)], [("o_mm1", 1)], chunks_=1)
                for h in range(2):
                    ph.step("pe", f"o_mm{h}", [("o_xt0", 0), ("out0", 0) if h else ("out1", 1)],
                            product(o_t, w_p2, feat, spread_ps, h * HALF, (h + 1) * HALF, chunks_=1))
                    ph.step("dve", f"out{h}", [(f"o_mm{h}", 0), ("ln", 2)], lambda q, h=h: V.tensor_tensor(
                        t13(q)[:, h * HALF:(h + 1) * HALF, :], grid(spread_ps, feat, HALF), bc(b_p2, feat, HALF), ALU.add))
                ph.step("pool", "out_x", [("out1", 0), ("own_x", 0)], lambda q: G.tensor_tensor(t13(q)[:], t13(q)[:], own_x[:, q.tri], ALU.add))
                layer_norm(ph, t13, [("out_x", 0)], lambda q: res[:, q.par], [("st_a", 2), ("t_tr1", 2)])
                ph.dma("act", "st_a", [("ln", 0)], lambda q: [S.dma_start(rows(x3, q), res[:, q.par])])
                table_out(w_g3, w_a3, f3, heads3, w3, tab3, lambda q: res[:, q.par])
            else:
                ph.step("dve", "out_b", [("agg", 0), ("relu", 1)], lambda q: V.tensor_tensor(t0[:], agg_v, bc(b_g3, f), ALU.add))
                ph.step("act", "relu", [("out_b", 0), ("x_read", 2)], lambda q: S.activation((t1, t2)[q.par][:], t0[:], ACT.Relu))

                def square(q):
                    for k in range(TILES):
                        i = S.activation(z[:, k, :], (t1, t2)[q.par][:, k, :], ACT.Square, accum_out=sq[:, k:k + 1])
                    return i
                ph.step("act", "sq", [("relu", 0), ("norm", 1)], square)
                ph.step("pool", "norm", [("sq", 0), ("norm_c", 1)], lambda q: G.tensor_tensor(norm_v[:, 0, :], sq[:], power[:, TILES:2 * TILES], ALU.pow))
                ph.step("dve", "norm_c", [("norm", 0), ("inv_n", 1)], lambda q: V.tensor_scalar(norm_v[:, 1, :], norm_v[:, 0, :], 1e-12, None, ALU.max))
                ph.step("dve", "inv_n", [("norm_c", 0), ("x_read", 1)], lambda q: V.reciprocal(norm_v[:, 2, :], norm_v[:, 1, :]))

                def add_x(q):
                    for k in range(TILES):
                        i = V.scalar_tensor_tensor(t3[:, k, :], (t1, t2)[q.par][:, k, :], norm_v[:, 2, k:k + 1], own_x[:, q.tri, k, :], ALU.mult, ALU.add)
                    return i
                ph.step("dve", "x_read", [("inv_n", 0), ("own_x", 0), ("ln", 1)], add_x)
                layer_norm(ph, lambda q: t3, [("x_read", 0)], lambda q: res[:, q.par], [("st_a", 2)])
                ph.dma("act", "st_a", [("ln", 0)], lambda q: [S.dma_start(rows(out, q), res[:, q.par])])
            ph.run(nc)

        hop(xw, "hop", [hop_a], first=True)
        hop(hop_a, "h1", [hop_b])
        hop(hop_b, "hop", [hop_a])
        hop(hop_a, "x1", [x1, tab1, recv1])
        gat(x1, tab1, feat, heads1, cols1, 1, "x2", v2=True)
        gat(x2, tab2, w2, heads2, cols2, 2, "project")
        gat(x3, tab3, w3, heads3, cols3, 2, "out")


INPUTS = ["x", "src", "dst", "L0_gnn_W1", "L0_gnn_b1", "L0_gnn_W2", "L0_gnn_b2", "L0_gnn_a", "L1_gnn_W_s", "L1_gnn_b_s",
          "L1_gnn_W_r", "L1_gnn_b_r", "L1_gnn_a_w", "L1_gnn_a_b", "L2_gnn_W", "L2_gnn_att_src", "L2_gnn_att_dst",
          "L2_gnn_bias", "L2_gnn_Wp", "L2_gnn_bp", "L3_gnn_W", "L3_gnn_att_src", "L3_gnn_att_dst", "L3_gnn_bias"]


def kernel(**inputs):
    import concourse.bacc as bacc
    from concourse.bass_utils import run_bass_kernel_spmd

    nc = bacc.Bacc("TRN2", target_bir_lowering=False, num_devices=1)
    arrays, args = {}, {}
    for name in INPUTS:
        v = np.ascontiguousarray(inputs[name])
        arrays["in_" + name] = v
        args[name] = nc.dram_tensor("in_" + name, v.shape, mybir.dt.from_np(v.dtype), kind="ExternalInput").ap()
    out = nc.dram_tensor("out", args["x"].shape, F32, kind="ExternalOutput").ap()
    build_program(nc, args, out)
    return run_bass_kernel_spmd(nc, [arrays], core_ids=[0]).results[0]["out"]
```
